# Optimizing a Trainium2 kernel written in Bass

```python
import numpy as np
import jax
import jax.numpy as jnp

def _softmax(x, axis=-1):
    return jax.nn.softmax(x, axis=axis)

def _gelu(x):
    return jax.nn.gelu(x, approximate=True)

def _silu(x):
    return jax.nn.silu(x)

def _sigmoid(x):
    return jax.nn.sigmoid(x)

def _layernorm(x, axis=-1, eps=1e-05):
    m = jnp.mean(x, axis=axis, keepdims=True)
    v = jnp.var(x, axis=axis, keepdims=True)
    return (x - m) / jnp.sqrt(v + eps)

def _scatter_add(tgt, idx, src, axis=0):
    return tgt.at[idx].add(src)

def _segment_sum(src, seg, n):
    return jax.ops.segment_sum(src, seg, n)
kernel_name = 'mk_conv_attn_hybrid_d4_conv_nhwc256_r2_a1ea43'

def setup_inputs(seed: int=0):
    np.random.seed(seed)
    _w = jnp.asarray

    def _rec_inputs():
        import jax
        import jax.numpy as jnp
        _gk = jax.random.key(seed)
        x = 7.22e-05 + 1 * jax.random.normal(jax.random.fold_in(_gk, 1), (8, 32, 32, 128), jnp.float32)
        return x
    x = _rec_inputs()

    def _L0_conv_setup():
        import jax, jax.numpy as jnp
        import numpy as np
        from jax import lax
        K = 3
        PAD = 1
        STRIDE = 1
        DIL = 1
        OFFSET_SIZE = 2 * K * K

        def _dcnv2(x, om_kernel, om_bias, kernel, bias):
            B, H, W, C = x.shape
            om = lax.conv_general_dilated(x, om_kernel, window_strides=(STRIDE, STRIDE), padding=((PAD, PAD), (PAD, PAD)), rhs_dilation=(DIL, DIL), dimension_numbers=('NHWC', 'HWIO', 'NHWC')) + om_bias
            OH, OW = (om.shape[1], om.shape[2])
            KK = K * K
            offset = om[..., :OFFSET_SIZE].reshape(B, OH, OW, KK, 2)
            mask = jax.nn.sigmoid(om[..., OFFSET_SIZE:]) * 2.0
            kk = jnp.arange(KK)
            ky = (kk // K).astype(jnp.float32)
            kx = (kk % K).astype(jnp.float32)
            base_y = jnp.arange(OH, dtype=jnp.float32)[:, None] * STRIDE - PAD + ky[None, :] * DIL
            base_x = jnp.arange(OW, dtype=jnp.float32)[:, None] * STRIDE - PAD + kx[None, :] * DIL
            py = base_y[None, :, None, :] + offset[..., 0]
            px = base_x[None, None, :, :] + offset[..., 1]
            y0 = jnp.floor(py)
            x0 = jnp.floor(px)
            wy1 = py - y0
            wy0 = 1.0 - wy1
            wx1 = px - x0
            wx0 = 1.0 - wx1
            bi = jnp.arange(B)[:, None, None, None]

            def gather(yi, xi):
                valid = (yi >= 0) & (yi <= H - 1) & (xi >= 0) & (xi <= W - 1)
                yc = jnp.clip(yi, 0, H - 1).astype(jnp.int32)
                xc = jnp.clip(xi, 0, W - 1).astype(jnp.int32)
                v = x[bi, yc, xc]
                return v * valid[..., None].astype(x.dtype)
            y1 = y0 + 1.0
            x1 = x0 + 1.0
            cols = gather(y0, x0) * (wy0 * wx0)[..., None] + gather(y0, x1) * (wy0 * wx1)[..., None] + gather(y1, x0) * (wy1 * wx0)[..., None] + gather(y1, x1) * (wy1 * wx1)[..., None]
            cols = cols * mask[..., None]
            out = cols.reshape(B, OH, OW, KK * C) @ kernel
            return out + bias
        key = jax.random.key(seed)
        k1, k2, k3, k4 = jax.random.split(key, 4)
        B, H, W, C = (8, 32, 32, 128)
        F = 128
        inputs = jax.random.normal(k1, (B, H, W, C), dtype=jnp.float32)
        om_kernel = jax.random.normal(k2, (K, K, C, OFFSET_SIZE * 3 // 2), dtype=jnp.float32) * 0.01
        om_bias = jnp.zeros((OFFSET_SIZE * 3 // 2,), dtype=jnp.float32)
        stdv = 1.0 / np.sqrt(K * K * C)
        kernel = jax.random.uniform(k3, (K * K * C, F), dtype=jnp.float32, minval=-stdv, maxval=stdv)
        bias = jax.random.normal(k4, (1, 1, 1, F), dtype=jnp.float32) * 0.01
        return {'inputs': inputs, 'om_kernel': om_kernel, 'om_bias': om_bias, 'kernel': kernel, 'bias': bias}
    _L0_conv_all = _L0_conv_setup()
    _L0_conv_in = {k: v for k, v in _L0_conv_all.items() if k in ('om_kernel', 'om_bias', 'kernel', 'bias')}
    del _L0_conv_all

    def _L1_conv_setup():
        import jax, jax.numpy as jnp
        import numpy as np
        NB_POOLS = 128
        B, H, W, C = (8, 32, 32, 128)
        key = jax.random.key(seed)
        x = jax.random.normal(key, (B, H, W, C), dtype=jnp.float32)
        return {'x': x}
    _L1_conv_all = _L1_conv_setup()
    _L1_conv_in = {k: v for k, v in _L1_conv_all.items() if k in ()}
    del _L1_conv_all

    def _L2_attn_setup():
        import jax, jax.numpy as jnp
        import numpy as np
        WINDOW_SIZES = (4, 16, 32)
        MEMORY_DIM = 128

        def _gather_patches(h, window):
            B, L, D = h.shape
            w = min(window, L)
            padded = jnp.pad(h, ((0, 0), (w - 1, 0), (0, 0)))
            idx = jnp.arange(L)[:, None] + jnp.arange(w)[None, :]
            return padded[:, idx]
        key = jax.random.key(seed)
        ks = jax.random.split(key, 9)
        d_model, mem = (128, MEMORY_DIM)
        s_in = 1.0 / np.sqrt(d_model)
        s_mem = 1.0 / np.sqrt(mem)
        return {'hidden_states': jax.random.normal(ks[0], (2, 2048, d_model), dtype=jnp.float32), 'Wq': jax.random.normal(ks[1], (d_model, mem), dtype=jnp.float32) * s_in, 'bq': jax.random.normal(ks[2], (mem,), dtype=jnp.float32) * 0.02, 'Wk': jax.random.normal(ks[3], (d_model, mem), dtype=jnp.float32) * s_in, 'bk': jax.random.normal(ks[4], (mem,), dtype=jnp.float32) * 0.02, 'Wv': jax.random.normal(ks[5], (d_model, mem), dtype=jnp.float32) * s_in, 'bv': jax.random.normal(ks[6], (mem,), dtype=jnp.float32) * 0.02, 'Wo': jax.random.normal(ks[7], (mem, d_model), dtype=jnp.float32) * s_mem, 'bo': jax.random.normal(ks[8], (d_model,), dtype=jnp.float32) * 0.02}
    _L2_attn_all = _L2_attn_setup()
    _L2_attn_in = {k: v for k, v in _L2_attn_all.items() if k in ('Wq', 'bq', 'Wk', 'bk', 'Wv', 'bv', 'Wo', 'bo')}
    del _L2_attn_all

    def _L2_ffn_setup():
        import jax, jax.numpy as jnp
        import numpy as np
        NUM_EXPERTS = 8
        TOP_K = 2
        B, S, D = (8, 4096, 128)

        def _moe(tokens, router_w, w1, b1, w2, b2):
            N = tokens.shape[0]
            E = router_w.shape[0]
            logits = tokens.astype(jnp.float32) @ router_w.astype(jnp.float32).T
            probs = jax.nn.softmax(logits, axis=-1)
            rw, re = jax.lax.top_k(probs, TOP_K)
            if TOP_K > 1:
                rw = rw / jnp.maximum(rw.sum(-1, keepdims=True), 1e-12)
            rw = rw.astype(tokens.dtype)
            combine = jnp.zeros((N, E), tokens.dtype).at[jnp.arange(N)[:, None], re].set(rw)
            out = tokens
            for e in range(E):
                h = jax.nn.gelu(tokens @ w1[e] + b1[e], approximate=False)
                y = h @ w2[e] + b2[e]
                out = out + combine[:, e:e + 1] * y
            return out
        key = jax.random.key(seed)
        ks = jax.random.split(key, 4)
        scale = 1.0 / np.sqrt(D).astype(np.float32)
        return {'input_embeddings': jax.random.normal(ks[0], (B, S, D), jnp.float32), 'router_w': jax.random.normal(ks[1], (NUM_EXPERTS, D), jnp.float32) * scale, 'w1': jax.random.normal(ks[2], (NUM_EXPERTS, D, D), jnp.float32) * scale, 'b1': jnp.zeros((NUM_EXPERTS, D), jnp.float32), 'w2': jax.random.normal(ks[3], (NUM_EXPERTS, D, D), jnp.float32) * scale, 'b2': jnp.zeros((NUM_EXPERTS, D), jnp.float32)}
    _L2_ffn_all = _L2_ffn_setup()
    _L2_ffn_in = {k: v for k, v in _L2_ffn_all.items() if k in ('router_w', 'w1', 'b1', 'w2', 'b2')}
    del _L2_ffn_all

    def _L3_attn_setup():
        import jax, jax.numpy as jnp
        import numpy as np
        D_MODEL = 128
        D_STATE = 32
        D_CONV = 4
        EXPAND = 2
        HEADDIM = 32
        D_INNER = EXPAND * D_MODEL
        NHEADS = D_INNER // HEADDIM
        CONV_DIM = D_INNER + 2 * D_STATE
        BATCH = 8
        SEQ = 2048

        def _rmsnorm(x, w, eps):
            return x * jax.lax.rsqrt(jnp.mean(x * x, axis=-1, keepdims=True) + eps) * w
        key = jax.random.key(seed)
        ks = jax.random.split(key, 6)
        x = jax.random.normal(ks[0], (BATCH, SEQ, D_MODEL), jnp.float32)
        d_in_proj = 2 * D_INNER + 2 * D_STATE + NHEADS
        W_in = jax.random.normal(ks[1], (d_in_proj, D_MODEL), jnp.float32) / np.sqrt(D_MODEL)
        conv_w = jax.random.normal(ks[2], (CONV_DIM, D_CONV), jnp.float32) / np.sqrt(D_CONV)
        conv_b = jnp.zeros((CONV_DIM,), jnp.float32)
        dt = jnp.exp(jax.random.uniform(ks[3], (NHEADS,), jnp.float32, np.log(0.001), np.log(0.1)))
        dt_bias = dt + jnp.log(-jnp.expm1(-dt))
        A_log = jnp.log(jax.random.uniform(ks[4], (NHEADS,), jnp.float32, 1.0, 16.0))
        Dp = jnp.ones((NHEADS,), jnp.float32)
        gnorm_w = jnp.ones((D_INNER,), jnp.float32)
        norm_w = jnp.ones((D_MODEL,), jnp.float32)
        W_out = jax.random.normal(ks[5], (D_MODEL, D_INNER), jnp.float32) / np.sqrt(D_INNER)
        return {'x': x, 'W_in': W_in, 'conv_w': conv_w, 'conv_b': conv_b, 'dt_bias': dt_bias, 'A_log': A_log, 'Dp': Dp, 'gnorm_w': gnorm_w, 'norm_w': norm_w, 'W_out': W_out}
    _L3_attn_all = _L3_attn_setup()
    _L3_attn_in = {k: v for k, v in _L3_attn_all.items() if k in ('W_in', 'conv_w', 'conv_b', 'dt_bias', 'A_log', 'Dp', 'gnorm_w', 'norm_w', 'W_out')}
    del _L3_attn_all

    def _L3_ffn_setup():
        import jax, jax.numpy as jnp
        import numpy as np
        N_EXPERTS = 8
        TOP_K = 2
        key = jax.random.key(seed)
        ks = jax.random.split(key, 5)
        B, T, C, E, H = (8, 1024, 128, 8, 341)
        scale = 1.0 / np.sqrt(C)
        return {'x': jax.random.normal(ks[0], (B, T, C), dtype=jnp.float32), 'router_w': jax.random.normal(ks[1], (E, C), dtype=jnp.float32) * scale, 'w1': jax.random.normal(ks[2], (E, H, C), dtype=jnp.float32) * scale, 'w2': jax.random.normal(ks[3], (E, C, H), dtype=jnp.float32) * (1.0 / np.sqrt(H)), 'w3': jax.random.normal(ks[4], (E, H, C), dtype=jnp.float32) * scale}
    _L3_ffn_all = _L3_ffn_setup()
    _L3_ffn_in = {k: v for k, v in _L3_ffn_all.items() if k in ('router_w', 'w1', 'w2', 'w3')}
    del _L3_ffn_all
    return {'x': x, 'L0_conv_om_kernel': _L0_conv_in['om_kernel'], 'L0_conv_om_bias': _L0_conv_in['om_bias'], 'L0_conv_kernel': _L0_conv_in['kernel'], 'L0_conv_bias': _L0_conv_in['bias'], 'L2_attn_Wq': _L2_attn_in['Wq'], 'L2_attn_bq': _L2_attn_in['bq'], 'L2_attn_Wk': _L2_attn_in['Wk'], 'L2_attn_bk': _L2_attn_in['bk'], 'L2_attn_Wv': _L2_attn_in['Wv'], 'L2_attn_bv': _L2_attn_in['bv'], 'L2_attn_Wo': _L2_attn_in['Wo'], 'L2_attn_bo': _L2_attn_in['bo'], 'L2_ffn_router_w': _L2_ffn_in['router_w'], 'L2_ffn_w1': _L2_ffn_in['w1'], 'L2_ffn_b1': _L2_ffn_in['b1'], 'L2_ffn_w2': _L2_ffn_in['w2'], 'L2_ffn_b2': _L2_ffn_in['b2'], 'L3_attn_W_in': _L3_attn_in['W_in'], 'L3_attn_conv_w': _L3_attn_in['conv_w'], 'L3_attn_conv_b': _L3_attn_in['conv_b'], 'L3_attn_dt_bias': _L3_attn_in['dt_bias'], 'L3_attn_A_log': _L3_attn_in['A_log'], 'L3_attn_Dp': _L3_attn_in['Dp'], 'L3_attn_gnorm_w': _L3_attn_in['gnorm_w'], 'L3_attn_norm_w': _L3_attn_in['norm_w'], 'L3_attn_W_out': _L3_attn_in['W_out'], 'L3_ffn_router_w': _L3_ffn_in['router_w'], 'L3_ffn_w1': _L3_ffn_in['w1'], 'L3_ffn_w2': _L3_ffn_in['w2'], 'L3_ffn_w3': _L3_ffn_in['w3']}

def reference(x, L0_conv_om_kernel, L0_conv_om_bias, L0_conv_kernel, L0_conv_bias, L2_attn_Wq, L2_attn_bq, L2_attn_Wk, L2_attn_bk, L2_attn_Wv, L2_attn_bv, L2_attn_Wo, L2_attn_bo, L2_ffn_router_w, L2_ffn_w1, L2_ffn_b1, L2_ffn_w2, L2_ffn_b2, L3_attn_W_in, L3_attn_conv_w, L3_attn_conv_b, L3_attn_dt_bias, L3_attn_A_log, L3_attn_Dp, L3_attn_gnorm_w, L3_attn_norm_w, L3_attn_W_out, L3_ffn_router_w, L3_ffn_w1, L3_ffn_w2, L3_ffn_w3):
    import jax
    import jax.numpy as jnp

    def _L0_conv_ref(inputs, om_kernel, om_bias, kernel, bias):
        import jax, jax.numpy as jnp
        import numpy as np
        from jax import lax
        K = 3
        PAD = 1
        STRIDE = 1
        DIL = 1
        OFFSET_SIZE = 2 * K * K

        def _dcnv2(x, om_kernel, om_bias, kernel, bias):
            B, H, W, C = x.shape
            om = lax.conv_general_dilated(x, om_kernel, window_strides=(STRIDE, STRIDE), padding=((PAD, PAD), (PAD, PAD)), rhs_dilation=(DIL, DIL), dimension_numbers=('NHWC', 'HWIO', 'NHWC')) + om_bias
            OH, OW = (om.shape[1], om.shape[2])
            KK = K * K
            offset = om[..., :OFFSET_SIZE].reshape(B, OH, OW, KK, 2)
            mask = jax.nn.sigmoid(om[..., OFFSET_SIZE:]) * 2.0
            kk = jnp.arange(KK)
            ky = (kk // K).astype(jnp.float32)
            kx = (kk % K).astype(jnp.float32)
            base_y = jnp.arange(OH, dtype=jnp.float32)[:, None] * STRIDE - PAD + ky[None, :] * DIL
            base_x = jnp.arange(OW, dtype=jnp.float32)[:, None] * STRIDE - PAD + kx[None, :] * DIL
            py = base_y[None, :, None, :] + offset[..., 0]
            px = base_x[None, None, :, :] + offset[..., 1]
            y0 = jnp.floor(py)
            x0 = jnp.floor(px)
            wy1 = py - y0
            wy0 = 1.0 - wy1
            wx1 = px - x0
            wx0 = 1.0 - wx1
            bi = jnp.arange(B)[:, None, None, None]

            def gather(yi, xi):
                valid = (yi >= 0) & (yi <= H - 1) & (xi >= 0) & (xi <= W - 1)
                yc = jnp.clip(yi, 0, H - 1).astype(jnp.int32)
                xc = jnp.clip(xi, 0, W - 1).astype(jnp.int32)
                v = x[bi, yc, xc]
                return v * valid[..., None].astype(x.dtype)
            y1 = y0 + 1.0
            x1 = x0 + 1.0
            cols = gather(y0, x0) * (wy0 * wx0)[..., None] + gather(y0, x1) * (wy0 * wx1)[..., None] + gather(y1, x0) * (wy1 * wx0)[..., None] + gather(y1, x1) * (wy1 * wx1)[..., None]
            cols = cols * mask[..., None]
            out = cols.reshape(B, OH, OW, KK * C) @ kernel
            return out + bias
        return _dcnv2(inputs, om_kernel, om_bias, kernel, bias)

    def _L1_conv_ref(x):
        import jax, jax.numpy as jnp
        import numpy as np
        NB_POOLS = 128
        B, H, W, C = (8, 32, 32, 128)
        b, h, w, c = x.shape
        m = h * w
        x3 = x.reshape(b, m, c)
        corr = jnp.einsum('bmc,bnc->bmn', x3, x3) / c
        corr = corr.reshape(b, h, w, m)
        x_sort = jnp.sort(corr, axis=-1)[..., ::-1]
        ranks = jnp.round(jnp.linspace(1.0, m - 1, NB_POOLS)).astype(jnp.int32)
        return x_sort[..., ranks]

    def _L2_attn_ref(hidden_states, Wq, bq, Wk, bk, Wv, bv, Wo, bo):
        import jax, jax.numpy as jnp
        import numpy as np
        WINDOW_SIZES = (4, 16, 32)
        MEMORY_DIM = 128

        def _gather_patches(h, window):
            B, L, D = h.shape
            w = min(window, L)
            padded = jnp.pad(h, ((0, 0), (w - 1, 0), (0, 0)))
            idx = jnp.arange(L)[:, None] + jnp.arange(w)[None, :]
            return padded[:, idx]
        scale = 1.0 / np.sqrt(MEMORY_DIM)
        q = hidden_states @ Wq + bq
        contexts = []
        for window in WINDOW_SIZES:
            patches = _gather_patches(hidden_states, window)
            keys = patches @ Wk + bk
            values = patches @ Wv + bv
            scores = jnp.einsum('bld,blwd->blw', q, keys) * scale
            attn = jax.nn.softmax(scores, axis=-1)
            contexts.append(jnp.einsum('blw,blwd->bld', attn, values))
        merged = contexts[0]
        for c in contexts[1:]:
            merged = merged + c
        merged = merged / len(contexts)
        return hidden_states + merged @ Wo + bo

    def _L2_ffn_ref(input_embeddings, router_w, w1, b1, w2, b2):
        import jax, jax.numpy as jnp
        import numpy as np
        NUM_EXPERTS = 8
        TOP_K = 2
        B, S, D = (8, 4096, 128)

        def _moe(tokens, router_w, w1, b1, w2, b2):
            N = tokens.shape[0]
            E = router_w.shape[0]
            logits = tokens.astype(jnp.float32) @ router_w.astype(jnp.float32).T
            probs = jax.nn.softmax(logits, axis=-1)
            rw, re = jax.lax.top_k(probs, TOP_K)
            if TOP_K > 1:
                rw = rw / jnp.maximum(rw.sum(-1, keepdims=True), 1e-12)
            rw = rw.astype(tokens.dtype)
            combine = jnp.zeros((N, E), tokens.dtype).at[jnp.arange(N)[:, None], re].set(rw)
            out = tokens
            for e in range(E):
                h = jax.nn.gelu(tokens @ w1[e] + b1[e], approximate=False)
                y = h @ w2[e] + b2[e]
                out = out + combine[:, e:e + 1] * y
            return out
        b, s, d = input_embeddings.shape
        tokens = input_embeddings.reshape(b * s, d)
        return _moe(tokens, router_w, w1, b1, w2, b2).reshape(b, s, d)

    def _L3_attn_ref(x, W_in, conv_w, conv_b, dt_bias, A_log, Dp, gnorm_w, norm_w, W_out):
        import jax, jax.numpy as jnp
        import numpy as np
        D_MODEL = 128
        D_STATE = 32
        D_CONV = 4
        EXPAND = 2
        HEADDIM = 32
        D_INNER = EXPAND * D_MODEL
        NHEADS = D_INNER // HEADDIM
        CONV_DIM = D_INNER + 2 * D_STATE
        BATCH = 8
        SEQ = 2048

        def _rmsnorm(x, w, eps):
            return x * jax.lax.rsqrt(jnp.mean(x * x, axis=-1, keepdims=True) + eps) * w
        Bsz, L, _ = x.shape
        xn = _rmsnorm(x, norm_w, jnp.finfo(x.dtype).eps)
        zxbcdt = jnp.einsum('bld,ed->ble', xn, W_in)
        z = zxbcdt[..., :D_INNER]
        xBC = zxbcdt[..., D_INNER:D_INNER + CONV_DIM]
        dt = zxbcdt[..., -NHEADS:]
        xpad = jnp.pad(xBC, ((0, 0), (D_CONV - 1, 0), (0, 0)))
        conv = sum((xpad[:, k:k + L, :] * conv_w[:, k] for k in range(D_CONV))) + conv_b
        xBC = jax.nn.silu(conv)
        xs = xBC[..., :D_INNER].reshape(Bsz, L, NHEADS, HEADDIM)
        Bm = xBC[..., D_INNER:D_INNER + D_STATE]
        Cm = xBC[..., D_INNER + D_STATE:]
        dt = jax.nn.softplus(dt + dt_bias)
        dA = jnp.exp(dt * -jnp.exp(A_log))

        def step(state, inp):
            dA_t, dt_t, B_t, C_t, x_t = inp
            state = state * dA_t[:, :, None, None] + (dt_t[:, :, None] * x_t)[..., None] * B_t[:, None, None, :]
            y = jnp.einsum('bhpn,bn->bhp', state, C_t)
            return (state, y)
        init = jnp.zeros((Bsz, NHEADS, HEADDIM, D_STATE), x.dtype)
        tm = lambda a: jnp.moveaxis(a, 1, 0)
        _, ys = jax.lax.scan(step, init, (tm(dA), tm(dt), tm(Bm), tm(Cm), tm(xs)))
        y = jnp.moveaxis(ys, 0, 1) + Dp[None, None, :, None] * xs
        y = y.reshape(Bsz, L, D_INNER)
        y = _rmsnorm(y * jax.nn.silu(z), gnorm_w, 1e-05)
        return x + jnp.einsum('ble,de->bld', y, W_out)

    def _L3_ffn_ref(x, router_w, w1, w2, w3):
        import jax, jax.numpy as jnp
        import numpy as np
        N_EXPERTS = 8
        TOP_K = 2
        B, T, C = x.shape
        flat = x.reshape(-1, C)
        logits = flat @ router_w.T
        probs = jax.nn.softmax(logits, axis=-1)
        topk_probs, topk_idx = jax.lax.top_k(probs, TOP_K)
        topk_probs = topk_probs / (jnp.sum(topk_probs, axis=-1, keepdims=True) + 1e-09)
        onehot = jax.nn.one_hot(topk_idx, N_EXPERTS, dtype=flat.dtype)
        gates = jnp.einsum('nk,nke->ne', topk_probs, onehot)
        h1 = jnp.einsum('nc,ehc->neh', flat, w1)
        h3 = jnp.einsum('nc,ehc->neh', flat, w3)
        h = jax.nn.silu(h1) * h3
        y = jnp.einsum('neh,ech->nec', h, w2)
        out = jnp.einsum('ne,nec->nc', gates, y)
        return out.reshape(B, T, C)

    def _gn(v, G=32, eps=1e-05):
        B_, H_, W_, C_ = v.shape
        g = v.reshape(B_, H_, W_, G, C_ // G)
        m = jnp.mean(g, axis=(1, 2, 4), keepdims=True)
        s = jnp.var(g, axis=(1, 2, 4), keepdims=True)
        return ((g - m) / jnp.sqrt(s + eps)).reshape(v.shape)

    def _ln_c(v, eps=1e-06):
        m = jnp.mean(v, axis=-1, keepdims=True)
        s = jnp.var(v, axis=-1, keepdims=True)
        return (v - m) / jnp.sqrt(s + eps)

    def _ln_t(v, eps=1e-05):
        m = jnp.mean(v, axis=-1, keepdims=True)
        s = jnp.var(v, axis=-1, keepdims=True)
        return (v - m) / jnp.sqrt(s + eps)

    def _to_tokens(v):
        B_, H_, W_, C_ = v.shape
        return v.reshape(B_, H_ * W_, C_)

    def _from_tokens(t, like):
        return t.reshape(like.shape)
    x = x + _L0_conv_ref(_gn(x), L0_conv_om_kernel, L0_conv_om_bias, L0_conv_kernel, L0_conv_bias)
    x = x + _L1_conv_ref(_gn(x))
    t = _to_tokens(x)
    t = t + _L2_attn_ref(_ln_t(t), L2_attn_Wq, L2_attn_bq, L2_attn_Wk, L2_attn_bk, L2_attn_Wv, L2_attn_bv, L2_attn_Wo, L2_attn_bo)
    t = t + _L2_ffn_ref(_ln_t(t), L2_ffn_router_w, L2_ffn_w1, L2_ffn_b1, L2_ffn_w2, L2_ffn_b2)
    t = t + _L3_attn_ref(_ln_t(t), L3_attn_W_in, L3_attn_conv_w, L3_attn_conv_b, L3_attn_dt_bias, L3_attn_A_log, L3_attn_Dp, L3_attn_gnorm_w, L3_attn_norm_w, L3_attn_W_out)
    t = t + _L3_ffn_ref(_ln_t(t), L3_ffn_router_w, L3_ffn_w1, L3_ffn_w2, L3_ffn_w3)
    x = _from_tokens(t, x)
    return x

_drawn_inputs = setup_inputs


def setup_inputs(seed=0):
    import zlib

    import numpy as np

    out = dict(_drawn_inputs(seed))
    spreads = {'L0_conv_om_bias': (0.0, 0.1),
     'L2_ffn_b1': (0.0, 0.392),
     'L2_ffn_b2': (0.0, 0.281),
     'L3_attn_conv_b': (0.0, 0.1),
     'L3_attn_Dp': (1.0, 0.2),
     'L3_attn_gnorm_w': (1.0, 0.2),
     'L3_attn_norm_w': (1.0, 0.2)}
    factors = {'L0_conv_bias': 3.106, 'L2_attn_bq': 8.0, 'L2_attn_bk': 8.0, 'L2_attn_bo': 3.269}
    for name, (base, spread) in spreads.items():
        noise = np.random.default_rng([zlib.crc32(name.encode()), seed]).standard_normal(out[name].shape)
        drawn = base * np.exp(spread * noise) if base else spread * noise
        out[name] = jnp.asarray(drawn.astype(out[name].dtype))
    for name, factor in factors.items():
        out[name] = (out[name] * factor).astype(out[name].dtype)
    return out
```

```python
import math
from contextlib import ExitStack

import numpy as np

import concourse.bass as bass
from concourse import mybir

IMAGES, HEIGHT, WIDTH, C = 8, 32, 32, 128
P = 128
TOK = HEIGHT * WIDTH
NT = TOK // P
ROWS = P // WIDTH
TAPS = 9
OM = 3 * TAPS
GROUP = 4
PADH = HEIGHT + 2
CELL = WIDTH + 2
QUAD = 4 * C
TG = 3
NG = NT * TAPS // TG
BACK = 32
KEYS = BACK + P
WINDOWS = (4, 16, 32)
E8 = 8
HEADS, HDIM, STATE = 8, 32, 32
INNER = HEADS * HDIM
XBC = INNER + 2 * STATE
CONVK = 4
ZDT = INNER + HEADS
HID = 341
HTILES = (128, 128, HID - 256)
HALF = 512
SORT_T = 4
RANKS = [int(r) for r in np.round(np.linspace(1.0, TOK - 1, C))]
GN_EPS, LN_EPS, RMS1_EPS, RMS2_EPS = 1e-5, 1e-5, float(np.finfo(np.float32).eps), 1e-5
NEG = -1e30
PIECE = "piece"


def rank_pieces():
    pieces = []
    for c, r in enumerate(RANKS):
        if pieces and r == pieces[-1][2] + 8 * pieces[-1][1]:
            pieces[-1][1] += 1
        else:
            pieces.append([c, 1, r])
    return pieces


def build(nc, A, IMGS=IMAGES, debug=None):
    F32, I32, U32 = mybir.dt.float32, mybir.dt.int32, mybir.dt.uint32
    ALU, ACT, AX = mybir.AluOpType, mybir.ActivationFunctionType, mybir.AxisListType
    ctx = ExitStack()
    with ctx:
        def sb(name, shape, dt=F32):
            return ctx.enter_context(nc.sbuf_tensor(name, shape, dt))

        ident = sb("ident", [P, P])
        gavg = sb("gavg", [P, P])
        tri = sb("tri", [P, P])
        ntri = sb("ntri", [P, P])
        later = sb("later", [P, P])
        future = sb("future", [P, P])
        ones = sb("ones", [P, P])
        band = sb("band", [P, len(WINDOWS), KEYS])
        base = sb("base", [P, 2, NT * TAPS])
        rev = sb("rev", [P, E8])
        eps_ln = sb("eps_ln", [P, 1])
        eps_rms1 = sb("eps_rms1", [P, 1])
        one_col = sb("one_col", [P, 1])
        om_w = sb("om_w", [P, TAPS, OM])
        om_b = sb("om_b", [1, OM])
        conv_w = sb("conv_w", [P, TAPS, C])
        conv_bias = sb("conv_bias", [1, C])
        wqkvo = sb("wqkvo", [P, 4, C])
        bqk = sb("bqk", [P, 2])
        bv_row = sb("bv_row", [1, C])
        bo_row = sb("bo_row", [1, C])
        router1 = sb("router1", [P, E8])
        router2 = sb("router2", [P, E8])
        b1 = sb("b1", [P, E8])
        b2 = sb("b2", [E8, C])
        w_zdt = sb("w_zdt", [P, ZDT])
        w_xbc = sb("w_xbc", [P, CONVK, XBC])
        cb_row = sb("cb_row", [1, XBC])
        cb_col = sb("cb_col", [STATE, 2])
        dt_bias = sb("dt_bias", [P, HEADS])
        neg_a = sb("neg_a", [P, HEADS])
        dskip = sb("dskip", [P, HEADS])
        gnorm = sb("gnorm", [P, 2])
        rms_w = sb("rms_w", [P, 1])
        w_out = sb("w_out", [P, 2, C])
        e1w = sb("e1w", [P, 2, 2, C])
        e2w = sb("e2w", [P, 2, 2 * HID + 3 * C])
        x_tok = sb("x_tok", [P, NT, C])
        xn_pad = sb("xn_pad", [P, 3, PADH, WIDTH])
        xn_tok = sb("xn_tok", [P, NT, C])
        x1_tok = xn_tok
        bst = sb("bst", [P, 2, 6])
        mv = sb("mv", [P, 8])
        oms = sb("oms", [P, NT, OM])
        mask = sb("mask", [P, NT, TAPS])
        idx = sb("idx", [P, NT * TAPS], U32)
        w4 = sb("w4", [P, NT * TAPS, 4])
        gath = sb("gath", [P, 2, TG, QUAD])
        diag = sb("diag", [P, 2, TG * 4, P])
        cols = sb("cols", [P, TAPS, P])
        colf = cols[:].rearrange("p k c -> p (k c)")
        n2 = 2 * NT * TAPS

        def pair(at):
            return colf[:, at * n2:(at + 1) * n2].rearrange("p (d n) -> p d n", d=2)

        pos, posi, cell, gt, wym = pair(0), pair(1).bitcast(I32), pair(2), pair(3), pair(4)
        frac = colf[:, 5 * n2:7 * n2].rearrange("p (s d n) -> p s d n", s=2, d=2)
        yn_t = sb("yn_t", [P, TOK])
        corr = sb("corr", [P, SORT_T, TOK])
        srt_a = sb("srt_a", [P, SORT_T, TOK])
        srt_b = sb("srt_b", [P, SORT_T, TOK])
        x2_tok = sb("x2_tok", [P, NT, C])
        t0 = sb("t0", [P, NT, C])
        t1 = sb("t1", [P, NT, C])
        u = sb("u", [P, NT, C])
        u_t = sb("u_t", [P, TOK + CONVK - 1])
        lnst = sb("lnst", [P, NT, 6])
        lnmv = sb("lnmv", [P, NT, 2])
        lnsd = sb("lnsd", [P, 2, NT])
        arena = sb("arena", [P, 10752])
        used = [0]

        def carve(n, *dims):
            a = arena[:, used[0]:used[0] + n]
            used[0] += n
            assert used[0] <= 10752, used
            if len(dims) == 2:
                return a.rearrange("p (a b) -> p a b", b=dims[1])
            if len(dims) == 3:
                return a.rearrange("p (a b c) -> p a b c", b=dims[1], c=dims[2])
            return a

        q_t = carve(TOK)
        k_t = carve(BACK + TOK)
        v_tok = carve((NT + 1) * C, NT + 1, C)
        ctx_t = carve(TOK)
        sm = [carve(3 * KEYS, 3, KEYS) for _ in range(2)]
        ex = [carve(3 * KEYS, 3, KEYS) for _ in range(2)]
        prob = carve(2 * P)
        prob_t = carve(2 * P)
        amax = [carve(3) for _ in range(2)]
        asum = [carve(3) for _ in range(2)]
        arec = carve(3)
        used[0] = 0
        gl = carve(NT * E8, NT, E8)
        gp = carve(NT * E8, NT, E8)
        gq = carve(NT * E8, NT, E8)
        gv = carve(NT * E8, NT, E8)
        oh1 = carve(NT * E8, NT, E8)
        oh2 = carve(NT * E8, NT, E8)
        gates = carve(NT * E8, NT, E8)
        gsm = carve(8 * NT, 8, NT)
        gates_t = carve(TOK)
        act_h = carve(2 * HALF, 2, HALF)
        gated_h = carve(2 * HALF, 2, HALF)
        gated_u = carve(2 * HALF, 2, HALF)
        used[0] = 0
        xbc = carve(NT * XBC, NT, XBC)
        zs = carve(NT * INNER, NT, INNER)
        ys = carve(NT * INNER, NT, INNER)
        b_t = carve(TOK)
        c_t = carve(TOK)
        decay = carve(HEADS * P, HEADS, P)
        mix = carve(HEADS * P, HEADS, P)
        dtr = sb("dtr", [P, NT, HEADS])
        dtx = sb("dtx", [P, 6, NT * HEADS])
        la = sb("la", [P, NT, HEADS])
        ecum = sb("ecum", [P, 3, NT * HEADS])
        xdt = sb("xdt", [P, INNER])
        xdr = sb("xdr", [P, INNER])
        yoff = sb("yoff", [P, INNER])
        state = sb("state", [STATE, INNER])
        rms = sb("rms", [P, 4, NT])
        y_t = arena[:, 0:2 * TOK].rearrange("p (a n) -> p a n", a=2)

        bank = [ctx.enter_context(nc.psum_tensor(f"bank{i}", [P, HALF], F32)) for i in range(8)]
        PA, PB = bank[0:4], bank[4:8]
        quads = nc.dram_tensor("quads", [CELL * CELL, QUAD], F32, kind="Internal").ap()

        PER = dict(
            x_in=16, x_t=2, gn_mom=4, gn_avg=4, gn_std=2, gn_scale=2, gn_out=2, om_done=1, om_sb=1, sig=1,
            xn_back=2, xn_tok=2, quad_out=16 * 32, idx=1, w4=1, gath0=16 * TG * NG // 2, gath1=16 * TG * NG // 2,
            diag=NG, colt=NG, cols=NG, conv=NT, x1=NT, corr_mm=NT, corr_sb=NT, corr_used=2, x2_copy=1, ranked=2,
            t_in=1, ln_v=4, ln_std=4, ln_u=4, ln_ut=6, ln_utsb=6,
            qkv=4, qkv_sb=5, score=NT, masked=NT, expd=NT, probd=NT, prob_ps=NT, prob_sb=NT, ctx_ps=NT, ctx_sb=NT,
            att_out=2, t1=2, e1_in0=16 * E8, e1_in1=16 * E8, logit=2, g_e=2, g_exp=2, gated=2, gt_ps=2, gt_sb=2,
            h_ps=16, gb_ps=16, gelu=16, gh=16, y1_ps=16, t2=2,
            rms_sq=2, rms_std=2, xn3=1, xn3_ps=2, xn3_t=2, z_ps=NT, z_sb=NT, x_ps=NT, xbc_sb=NT, bc_ps=4, bc_sb=4,
            dt_abs=1, dt_exp=1, dt_w=1, dt_ln=1, la=1, cum=1, ecum=1, seg=NT, decay=NT, cbt=NT, mix=NT,
            xdr=NT, y_ps=NT, ds_ps=NT, y_sb=NT, state=NT, yn=1, yt_ps=4, yt_sb=4, o_ps=2, t3=1,
            e2_in0=16 * 5 * E8 // 2, e2_in1=16 * 5 * E8 // 2, gb2=16, gu=16, h1_ps=48, h3_ps=48, silu=48, hh=48, y2_ps=48, out_sb=2, out=16,
        )
        PER.update(CHAIN_N)
        sem = {n: ctx.enter_context(nc.semaphore(n)) for n in PER}
        loaded = ctx.enter_context(nc.semaphore("loaded"))
        prep = ctx.enter_context(nc.semaphore("prep"))
        n_loads = [0]

        def upto(name, i, k=None):
            return i * PER[name] + (PER[name] if k is None else k)

        passed = ctx.enter_context(nc.semaphore("passed"))

        def settle(eng):
            eng.sem_inc(passed, 1)

        class Chain:

            def __init__(self, eng, name, i):
                self.eng, self.name, self.i, self.n = eng, name, i, 0

            def __call__(self, ins, name=None):
                ins.then_inc(sem[self.name], 1)
                self.n += 1
                self.eng.wait_ge(sem[self.name], upto(self.name, self.i, self.n))
                if name:
                    self.eng.sem_inc(sem[name], 1)

            def end(self):
                assert self.n == PER[self.name], (self.name, self.n)

        def bc(ap, *shape):
            return ap.to_broadcast(list(shape))

        V, T, SC, G = nc.vector, nc.tensor, nc.scalar, nc.gpsimd

        def sp_load(sp):
            def load(dst, src):
                sp.dma_start(dst, src).then_inc(loaded, 16)
                n_loads[0] += 1
            for dst, name in ((ident, "c_ident"), (gavg, "c_gavg"), (tri, "c_tri"), (ntri, "c_ntri"),
                              (later, "c_later"), (future, "c_future")):
                load(dst[:], A[name])
            load(band[:], A["c_band"])
            load(base[:], A["c_base"])
            load(rev[:], A["c_rev"])
            load(om_w[:], A["L0_conv_om_kernel"].rearrange("a b c o -> c (a b) o"))
            load(om_b[:], A["L0_conv_om_bias"].rearrange("(a o) -> a o", a=1))
            load(conv_w[:], A["L0_conv_kernel"].rearrange("(t c) f -> c t f", c=C))
            load(conv_bias[:], A["L0_conv_bias"].rearrange("a b c f -> (a b c) f"))
            for n, w in enumerate("qkvo"):
                load(wqkvo[:, n], A["L2_attn_W" + w])
            load(bqk[:, 0:1], A["L2_attn_bq"].rearrange("(c a) -> c a", a=1))
            load(bqk[:, 1:2], A["L2_attn_bk"].rearrange("(c a) -> c a", a=1))
            load(bv_row[:], A["L2_attn_bv"].rearrange("(a c) -> a c", a=1))
            load(bo_row[:], A["L2_attn_bo"].rearrange("(a c) -> a c", a=1))
            load(router1[:], A["router1_t"])
            load(router2[:], A["router2_t"])
            load(b1[:], A["b1_t"])
            load(b2[:], A["L2_ffn_b2"])
            load(w_zdt[:], A["w_zdt_t"])
            for k in range(CONVK):
                load(w_xbc[:, k], A["w_xbc_t"])
            load(cb_row[:], A["L3_attn_conv_b"].rearrange("(a c) -> a c", a=1))
            load(cb_col[:], A["cb_bc"])
            load(dt_bias[:], A["L3_attn_dt_bias"].partition_broadcast(P))
            load(neg_a[:], A["L3_attn_A_log"].partition_broadcast(P))
            load(dskip[:], A["L3_attn_Dp"].partition_broadcast(P))
            load(gnorm[:], A["gnorm_t"])
            load(rms_w[:], A["L3_attn_norm_w"].rearrange("(c a) -> c a", a=1))
            load(w_out[:], A["w_out_t"])
            load(gath[:].rearrange("p a b q -> p (a b q)")[:, 0:CONVK * XBC],
                 A["conv_w_t"].rearrange("a b -> (a b)").partition_broadcast(P))

        def sp_zero_quads(sp):
            sp.wait_ge(prep, 1)
            flat = quads.rearrange("a b -> (a b)").rearrange("(p n) -> p n", p=P)
            n = flat.shape[1]
            step = SORT_T * TOK
            za = srt_a[:].rearrange("p a b -> p (a b)")
            for o in range(0, n, step):
                w = min(step, n - o)
                sp.dma_start(flat[:, o:o + w], za[:, 0:w]).then_inc(loaded, 16)
                n_loads[0] += 1

        def dve_prep(dve):
            V.memset(srt_a[:], 0.0)
            V.memset(ones[:], 1.0)
            V.memset(xn_pad[:], 0.0)
            V.memset(u_t[:, 0:CONVK - 1], 0.0)
            V.memset(eps_ln[:], LN_EPS)
            V.memset(one_col[:], 1.0)
            V.memset(eps_rms1[:], RMS1_EPS).then_inc(prep, 1)
            dve.wait_ge(loaded, 16 * n_loads[0])
            cw = gath[:].rearrange("p a b q -> p (a b q)")[:, 0:CONVK * XBC]
            V.tensor_tensor(w_xbc[:].rearrange("p k c -> p (k c)"), w_xbc[:].rearrange("p k c -> p (k c)"), cw,
                            ALU.mult).then_inc(prep, 1)
            dve.wait_ge(prep, 3)
            V.tensor_scalar(neg_a[:], neg_a[:], -1.0, None, ALU.mult).then_inc(prep, 1)
            dve.wait_ge(prep, 4)

        def act_prep(act):
            act.wait_ge(loaded, 16 * n_loads[0])
            act.wait_ge(prep, 2)
            SC.activation(neg_a[:], neg_a[:], ACT.Exp).then_inc(prep, 1)
            act.wait_ge(prep, 4)

        def others_prep(eng):
            eng.wait_ge(loaded, 16 * n_loads[0])
            eng.wait_ge(prep, 4)

        def win(t, dy=1, dx=1):
            return xn_pad[:, dx, ROWS * t + dy:ROWS * t + dy + ROWS].rearrange("p y x -> p (y x)")

        def sp_pre(sp, i):
            sp.wait_ge(sem["conv"], upto("conv", i, 0))
            settle(sp)
            sp.dma_start(x_tok[:], A["x"][bass.ds(i, 1)].rearrange("a (t r) w c -> (a r w) t c", t=NT)).then_inc(sem["x_in"], 16)
            sp.wait_ge(sem["xn_tok"], upto("xn_tok", i, 2))
            settle(sp)
            sp.wait_ge(sem["gath0"], upto("gath0", i, 0))
            settle(sp)
            sp.wait_ge(sem["gath1"], upto("gath1", i, 0))
            settle(sp)
            q = quads.rearrange("(y x) (s c) -> y x s c", x=CELL, c=C)
            for t in range(NT):
                for dy in range(2):
                    for dx in range(2):
                        for_rows = q[ROWS * t + 1 - dy:ROWS * t + 1 - dy + ROWS, 1 - dx:1 - dx + WIDTH, 2 * dy + dx]
                        sp.dma_start(for_rows, xn_tok[:, t]).then_inc(sem["quad_out"], 16)

        def pe_gn(pe, i, n, src):
            for t in range(NT):
                ins = T.transpose(PA[t // 4][:, (t % 4) * P:(t % 4 + 1) * P], src[:, t], ident[:])
            ins.then_inc(sem["x_t"], 1)
            for k in range(2):
                pe.wait_ge(sem["gn_mom"], upto("gn_mom", i, 2 * n + k + 1))
                T.matmul(PA[2][:, 0:1], gavg[:], mv[:, (0, 4)[k]:(0, 4)[k] + 1], start=True, stop=True).then_inc(sem["gn_avg"], 1)

        def dve_gn(dve, i, n, link):
            dve.wait_ge(sem["x_t"], upto("x_t", i, n + 1))
            for h in range(2):
                ins = V.bn_stats(bst[:, h], PA[h][:])
                if h:
                    link(ins)
            settle(dve)
            link(V.bn_aggr(mv[:, 0:2], bst[:]), "gn_mom")
            yield
            dve.wait_ge(sem["gn_avg"], upto("gn_avg", i, 2 * n + 1))
            link(V.tensor_copy(mv[:, 2:3], PA[2][:, 0:1]))
            link(V.tensor_tensor(mv[:, 3:4], mv[:, 0:1], mv[:, 2:3], ALU.subtract))
            V.scalar_tensor_tensor(mv[:, 4:5], mv[:, 3:4], mv[:, 3:4], mv[:, 1:2], ALU.mult, ALU.add).then_inc(sem["gn_mom"], 1)
            yield
            dve.wait_ge(sem["gn_std"], upto("gn_std", i, n + 1))
            link(V.reciprocal(mv[:, 6:7], mv[:, 5:6]))
            V.scalar_tensor_tensor(mv[:, 7:8], mv[:, 2:3], -1.0, mv[:, 6:7], ALU.mult, ALU.mult).then_inc(sem["gn_scale"], 1)

        def act_gn(act, i, n):
            act.wait_ge(sem["gn_avg"], upto("gn_avg", i, 2 * n + 2))
            SC.activation(mv[:, 5:6], PA[2][:, 0:1], ACT.Sqrt, bias=eps_ln[:, 0:1]).then_inc(sem["gn_std"], 1)
            act.wait_ge(sem["gn_scale"], upto("gn_scale", i, n + 1))
            for h in range(2):
                if n == 0:
                    img = PA[h][:].rearrange("p (y x) -> p y x", x=WIDTH)
                    rows = xn_pad[:, :, 1 + 16 * h:17 + 16 * h]
                    moves = [(rows[:, 1], img), (rows[:, 0, :, 1:WIDTH], img[:, :, 0:WIDTH - 1]),
                             (rows[:, 2, :, 0:WIDTH - 1], img[:, :, 1:WIDTH])]
                else:
                    moves = [(yn_t[:, h * HALF:(h + 1) * HALF], PA[h][:])]
                for dst, src in moves:
                    ins = SC.activation(dst, src, ACT.Identity, bias=mv[:, 7:8], scale=mv[:, 6:7])
            ins.then_inc(sem["gn_out"], 1)

        def pe_pre(pe, i):
            pe.wait_ge(sem["x_in"], upto("x_in", i))
            pe.wait_ge(sem["corr_sb"], upto("corr_sb", i, 0))
            pe_gn(pe, i, 0, x_tok)
            yield
            pe.wait_ge(sem["gn_out"], upto("gn_out", i, 1))
            om = PA[3][:, 0:NT * OM].rearrange("p (t o) -> p t o", o=OM)
            T.matmul(om, ones[0:1, :], om_b[:].unsqueeze(1).to_broadcast([1, NT, OM]), start=True, stop=False)
            for t in range(NT):
                for k in range(TAPS):
                    ins = T.matmul(om[:, t], win(t, k // 3, k % 3), om_w[:, k], start=False,
                                   stop=(t == NT - 1 and k == TAPS - 1))
            ins.then_inc(sem["om_done"], 1)
            for t in range(NT):
                ins = T.transpose(PA[t // 4][:, (t % 4) * P:(t % 4 + 1) * P], win(t), ident[:])
                if t % 4 == 3:
                    ins.then_inc(sem["xn_back"], 1)
            yield
            for g in range(NG):
                t, part = divmod(g, TAPS // TG)
                pe.wait_ge(sem["gath%d" % (g % 2)], upto("gath%d" % (g % 2), i, 16 * TG * (g // 2 + 1)))
                pe.wait_ge(sem["diag"], upto("diag", i, g + 1))
                if g < 2:
                    pe.wait_ge(sem["xn_tok"], upto("xn_tok", i, g + 1))
                else:
                    pe.wait_ge(sem["cols"], upto("cols", i, g - 1))
                for k in range(TG):
                    for s in range(4):
                        ins = T.matmul(PA[g % 2][:, k * P:(k + 1) * P], gath[:, g % 2, k, s * C:(s + 1) * C],
                                       diag[:, g % 2, 4 * k + s], start=(s == 0), stop=(s == 3))
                ins.then_inc(sem["colt"], 1)
                if part == TAPS // TG - 1:
                    pe.wait_ge(sem["cols"], upto("cols", i, g + 1))
                    if t == 0:
                        pe.wait_ge(sem["om_sb"], upto("om_sb", i))
                        pe.wait_ge(sem["sig"], upto("sig", i))
                    if t >= 2:
                        pe.wait_ge(sem["x1"], upto("x1", i, t - 1))
                    out = PA[2 + t % 2][:, 0:C]
                    T.matmul(out, ident[:], x_tok[:, t], start=True, stop=False)
                    T.matmul(out, ones[0:1, :], conv_bias[:], start=False, stop=False)
                    for k in range(TAPS):
                        ins = T.matmul(out, cols[:, k], conv_w[:, k], start=False, stop=(k == TAPS - 1))
                    ins.then_inc(sem["conv"], 1)
                yield
            pe.wait_ge(sem["x1"], upto("x1", i))
            pe_gn(pe, i, 1, x1_tok)
            yield
            pe.wait_ge(sem["gn_out"], upto("gn_out", i, 2))

        def pe_corr(pe, i, h2):
            for t in range(SORT_T * h2, SORT_T * (h2 + 1)):
                if t >= 2:
                    pe.wait_ge(sem["corr_sb"], upto("corr_sb", i, t - 1))
                for h in range(2):
                    ins = T.matmul(PA[2 * (t % 2) + h][:], yn_t[:, t * P:(t + 1) * P], yn_t[:, h * HALF:(h + 1) * HALF],
                                   start=True, stop=True)
                ins.then_inc(sem["corr_mm"], 1)
                yield

        def act_pre(act, i):
            act_gn(act, i, 0)
            yield
            act.wait_ge(sem["om_done"], upto("om_done", i))
            om = PA[3][:, 0:NT * OM].rearrange("p (t o) -> p t o", o=OM)
            SC.activation(oms[:], om, ACT.Identity).then_inc(sem["om_sb"], 1)
            SC.activation(mask[:], om[:, :, 2 * TAPS:OM], ACT.Sigmoid).then_inc(sem["sig"], 1)
            for h in range(2):
                act.wait_ge(sem["xn_back"], upto("xn_back", i, h + 1))
                if h == 0:
                    act.wait_ge(sem["quad_out"], upto("quad_out", i, 0))
                SC.activation(xn_tok[:, 4 * h:4 * h + 4].rearrange("p t c -> p (t c)"), PA[h][:], ACT.Identity).then_inc(sem["xn_tok"], 1)
            yield
            for g in range(NG):
                t, part = divmod(g, TAPS // TG)
                act.wait_ge(sem["colt"], upto("colt", i, g + 1))
                if part == 0 and t:
                    act.wait_ge(sem["conv"], upto("conv", i, t))
                SC.activation(cols[:, TG * part:TG * (part + 1)].rearrange("p k c -> p (k c)"),
                                   PA[g % 2][:, 0:TG * P], ACT.Identity).then_inc(sem["cols"], 1)
                if part == TAPS // TG - 1:
                    act.wait_ge(sem["conv"], upto("conv", i, t + 1))
                    if t == 0:
                        act.wait_ge(sem["quad_out"], upto("quad_out", i))
                    SC.activation(x1_tok[:, t], PA[2 + t % 2][:, 0:C], ACT.Identity).then_inc(sem["x1"], 1)
                yield
            act_gn(act, i, 1)
            yield

        def act_corr(act, i, h2):
            for t in range(SORT_T * h2, SORT_T * (h2 + 1)):
                act.wait_ge(sem["corr_mm"], upto("corr_mm", i, t + 1))
                if t % SORT_T == 0:
                    act.wait_ge(sem["corr_used"], upto("corr_used", i, h2))
                for h in range(2):
                    ins = SC.activation(corr[:, t % SORT_T, h * HALF:(h + 1) * HALF], PA[2 * (t % 2) + h][:],
                                        ACT.Identity, scale=1.0 / C)
                ins.then_inc(sem["corr_sb"], 1)
                yield

        def dve_pre(dve, i):
            link = Chain(dve, "dve_pre", i)
            yield from dve_gn(dve, i, 0, link)
            yield PIECE
            dve.wait_ge(sem["om_sb"], upto("om_sb", i))
            off = oms[:, :, 0:2 * TAPS].rearrange("p t (k d) -> p t k d", d=2)
            for d in range(2):
                ins = V.tensor_tensor(pos[:, d].rearrange("p (t k) -> p t k", k=TAPS),
                                      base[:, d].rearrange("p (t k) -> p t k", k=TAPS), off[:, :, :, d], ALU.add)
            link(ins)
            link(V.tensor_scalar(pos[:], pos[:], 0.0, float(HEIGHT + 1), ALU.max, ALU.min))
            link(V.tensor_copy(posi[:], pos[:]))
            link(V.tensor_copy(cell[:], posi[:]))
            link(V.tensor_tensor(gt[:], cell[:], pos[:], ALU.is_gt))
            link(V.tensor_tensor(cell[:], cell[:], gt[:], ALU.subtract))
            dve.wait_ge(sem["gath0"], upto("gath0", i, 0))
            dve.wait_ge(sem["gath1"], upto("gath1", i, 0))
            V.scalar_tensor_tensor(idx[:], cell[:, 0], float(CELL), cell[:, 1], ALU.mult, ALU.add).then_inc(sem["idx"], 1)
            link(V.tensor_tensor(frac[:, 1], pos[:], cell[:], ALU.subtract))
            link(V.tensor_scalar(frac[:, 0], frac[:, 1], -1.0, 1.0, ALU.mult, ALU.add))
            dve.wait_ge(sem["sig"], upto("sig", i))
            for r in range(2):
                ins = V.scalar_tensor_tensor(wym[:, r], mask[:].rearrange("p t k -> p (t k)"), 2.0, frac[:, r, 0],
                                             ALU.mult, ALU.mult)
            link(ins)
            dve.wait_ge(sem["diag"], upto("diag", i, 0))
            for r in range(2):
                for c in range(2):
                    ins = V.tensor_tensor(w4[:, :, 2 * r + c], wym[:, r], frac[:, c, 1], ALU.mult)
            ins.then_inc(sem["w4"], 1)
            yield PIECE
            for g in range(NG):
                yield PIECE
            yield from dve_gn(dve, i, 1, link)
            link.end()
            yield PIECE
            for t in range(SORT_T):
                yield PIECE

        def pool_pre(pool, i):
            def gather(g):
                if g >= 2:
                    pool.wait_ge(sem["colt"], upto("colt", i, g - 1))
                    settle(pool)
                for k in range(TG):
                    pool.indirect_dma_start(gath[:, g % 2, k], None, quads,
                                            bass.IndirectOffsetOnAxis(idx[:, TG * g + k:TG * g + k + 1], 0)
                                                 ).then_inc(sem["gath%d" % (g % 2)], 16)

            for _ in range(2):
                yield
            pool.wait_ge(sem["idx"], upto("idx", i))
            settle(pool)
            pool.wait_ge(sem["quad_out"], upto("quad_out", i))
            settle(pool)
            gather(0)
            gather(1)
            pool.wait_ge(sem["w4"], upto("w4", i))
            settle(pool)
            for g in range(NG):
                if g >= 2:
                    pool.wait_ge(sem["colt"], upto("colt", i, g - 1))
                    settle(pool)
                w = w4[:, TG * g:TG * (g + 1)].rearrange("p k s -> p (k s)")
                G.tensor_tensor(diag[:, g % 2], ident[:].unsqueeze(1).to_broadcast([P, 4 * TG, P]),
                                     w.unsqueeze(2).to_broadcast([P, 4 * TG, P]), ALU.mult).then_inc(sem["diag"], 1)
                if g + 2 < NG:
                    gather(g + 2)
                yield
            for _ in range(1 + SORT_T):
                yield

        def dve_sort(dve, i, h, link):
            dve.wait_ge(sem["corr_sb"], upto("corr_sb", i, SORT_T * (h + 1)))
            src, n, stage = corr, TOK, 0
            bufs = (srt_a, srt_b)
            m = 2
            while m <= n:
                k = m // 2
                first = True
                while k >= 1:
                    if m == n and k <= 4:
                        break
                    dst = bufs[stage % 2]
                    size = 2 * k if not first else m
                    x = src[:].rearrange("p g (b m) -> p (g b) m", m=size)
                    y = dst[:].rearrange("p g (b m) -> p (g b) m", m=size)
                    lo, hi = x[:, :, 0:k], x[:, :, k:2 * k]
                    if first:
                        hi = hi[:, :, ::-1]
                    V.tensor_tensor(y[:, :, 0:k], lo, hi, ALU.max)
                    link(V.tensor_tensor(y[:, :, k:2 * k], lo, hi, ALU.min), None if stage else "corr_used")
                    yield
                    src = dst
                    stage += 1
                    first = False
                    k //= 2
                m *= 2
            for k in (4, 2, 1):
                dst = bufs[stage % 2]
                last = k == 1
                for c, cnt, r in rank_pieces():
                    base_r = r // (2 * k) * (2 * k)
                    side = ALU.max if (r % (2 * k)) < k else ALU.min
                    lo = bass_slice(src, base_r, cnt, k)
                    hi = bass_slice(src, base_r + k, cnt, k)
                    if last:
                        out = dst[:, :, c:c + cnt].unsqueeze(3)
                    else:
                        out = bass_slice(dst, r // k * k, cnt, k)
                    ins = V.tensor_tensor(out, lo, hi, side)
                link(ins)
                yield
                src = dst
                stage += 1
            if h == 0:
                dve.wait_ge(sem["x2_copy"], upto("x2_copy", i))
            x2 = x2_tok[:, SORT_T * h:SORT_T * (h + 1)]
            link(V.tensor_tensor(x2, x2, src[:, :, 0:C], ALU.add), "ranked")

        def bass_slice(buf, start, cnt, k):
            cells = buf[:].rearrange("p g (b e) -> p g b e", e=8)
            return cells[:, :, start // 8:start // 8 + cnt, start % 8:start % 8 + k]

        def ln_stats(dve, i, n, src, link):
            for t in range(NT):
                ins = V.bn_stats(lnst[:, t], src[:, t])
            link(ins)
            settle(dve)
            for t in range(NT):
                ins = V.bn_aggr(lnmv[:, t], lnst[:, t:t + 1])
            link(ins)
            link(V.tensor_scalar(lnsd[:, 0], lnmv[:, :, 1], LN_EPS, None, ALU.add), "ln_v")
            yield
            dve.wait_ge(sem["ln_std"], upto("ln_std", i, n + 1))
            link(V.reciprocal(lnsd[:, 1], lnsd[:, 0]))
            for t in range(NT):
                ins = V.tensor_scalar(u[:, t], src[:, t], lnmv[:, t, 0:1], lnsd[:, 1, t:t + 1], ALU.subtract, ALU.mult)
            ins.then_inc(sem["ln_u"], 1)

        def act_ln(act, i, n, transposed=True):
            act.wait_ge(sem["ln_v"], upto("ln_v", i, n + 1))
            SC.activation(lnsd[:, 0], lnsd[:, 0], ACT.Sqrt).then_inc(sem["ln_std"], 1)
            if transposed:
                for h in range(2):
                    act.wait_ge(sem["ln_ut"], upto("ln_ut", i, 2 * (n - n // 3) + h + 1))
                    SC.activation(u_t[:, 3 + h * HALF:3 + (h + 1) * HALF], PB[h][:], ACT.Identity).then_inc(sem["ln_utsb"], 1)

        def pe_ln(pe, i, n):
            pe.wait_ge(sem["ln_u"], upto("ln_u", i, n + 1))
            for t in range(NT):
                ins = T.transpose(PB[t // 4][:, (t % 4) * P:(t % 4 + 1) * P], u[:, t], ident[:])
                if t % 4 == 3:
                    ins.then_inc(sem["ln_ut"], 1)

        def utile(t):
            return u_t[:, 3 + t * P:3 + (t + 1) * P]

        def uhalf(h):
            return u_t[:, 3 + h * HALF:3 + (h + 1) * HALF]

        def flat4(buf, h):
            return buf[:, 4 * h:4 * h + 4].rearrange("p t c -> p (t c)")

        def row4(row):
            return row.unsqueeze(1).to_broadcast([1, 4, C])

        SCALE = 1.0 / math.sqrt(C)

        def pe_att(pe, i):
            pe_ln(pe, i, 0)
            yield
            pe.wait_ge(sem["ln_utsb"], upto("ln_utsb", i, 2))
            for h in range(2):
                ins = T.matmul(PB[h][:], wqkvo[:, 0], uhalf(h), start=True, stop=True)
            ins.then_inc(sem["qkv"], 1)
            for h in range(2):
                ins = T.matmul(PB[2 + h][:], wqkvo[:, 1], uhalf(h), start=True, stop=True)
            ins.then_inc(sem["qkv"], 1)
            yield
            pe.wait_ge(sem["qkv_sb"], upto("qkv_sb", i, 1))
            for h in range(2):
                T.matmul(PB[h][:], ones[0:1, :], row4(bv_row[:]), start=True, stop=False)
                for t in range(4):
                    ins = T.matmul(PB[h][:, t * P:(t + 1) * P], utile(4 * h + t), wqkvo[:, 2], start=False,
                                   stop=(t == 3))
            ins.then_inc(sem["qkv"], 1)
            pe.wait_ge(sem["qkv_sb"], upto("qkv_sb", i, 2))
            T.matmul(PB[2][:, 0:C], ones[0:1, :], bv_row[:], start=True, stop=True).then_inc(sem["qkv"], 1)
            yield
            pe.wait_ge(sem["qkv_sb"], upto("qkv_sb", i, 4))

            def scores(t):
                if t >= 2:
                    pe.wait_ge(sem["masked"], upto("masked", i, t - 1))
                T.matmul(PB[t % 2][:, 0:KEYS], q_t[:, t * P:(t + 1) * P], k_t[:, t * P:t * P + KEYS],
                              start=True, stop=True).then_inc(sem["score"], 1)
            scores(0)
            yield
            for t in range(1, NT + 2):
                if t < NT:
                    scores(t)
                if 2 <= t:
                    n = t - 2
                    pe.wait_ge(sem["probd"], upto("probd", i, n + 1))
                    if n:
                        pe.wait_ge(sem["prob_sb"], upto("prob_sb", i, n))
                    for s in range(2):
                        ins = T.transpose(PB[2][:, s * P:(s + 1) * P], prob[:, s * P:(s + 1) * P], ident[:])
                    ins.then_inc(sem["prob_ps"], 1)
                    pe.wait_ge(sem["prob_sb"], upto("prob_sb", i, n + 1))
                    if n:
                        pe.wait_ge(sem["ctx_sb"], upto("ctx_sb", i, n))
                    for s in range(2):
                        ins = T.matmul(PB[3][:, 0:P], v_tok[:, n + s], prob_t[:, s * P:(s + 1) * P],
                                       start=(s == 0), stop=(s == 1))
                    ins.then_inc(sem["ctx_ps"], 1)
                yield
            pe.wait_ge(sem["ctx_sb"], upto("ctx_sb", i))
            for h in range(2):
                T.matmul(PB[h][:], ident[:], flat4(t0, h), start=True, stop=False)
                T.matmul(PB[h][:], ident[:], flat4(u, h), start=False, stop=False)
                T.matmul(PB[h][:], ones[0:1, :], row4(bo_row[:]), start=False, stop=False)
                for t in range(4):
                    n = 4 * h + t
                    ins = T.matmul(PB[h][:, t * P:(t + 1) * P], ctx_t[:, n * P:(n + 1) * P], wqkvo[:, 3],
                                   start=False, stop=(t == 3))
                ins.then_inc(sem["att_out"], 1)
            yield

        def act_att(act, i):
            act_ln(act, i, 0)
            yield
            act.wait_ge(sem["qkv"], upto("qkv", i, 1))
            for h in range(2):
                ins = SC.activation(q_t[:, h * HALF:(h + 1) * HALF], PB[h][:], ACT.Identity, bias=bqk[:, 0:1])
            ins.then_inc(sem["qkv_sb"], 1)
            act.wait_ge(sem["qkv"], upto("qkv", i, 2))
            for h in range(2):
                SC.activation(k_t[:, BACK + h * HALF:BACK + (h + 1) * HALF], PB[2 + h][:], ACT.Identity,
                              bias=bqk[:, 1:2])
            SC.activation(k_t[:, 0:BACK], ident[:, 0:BACK], ACT.Identity, bias=bqk[:, 1:2], scale=0.0).then_inc(sem["qkv_sb"], 1)
            yield
            act.wait_ge(sem["qkv"], upto("qkv", i, 3))
            for h in range(2):
                ins = SC.activation(v_tok[:, 1 + 4 * h:5 + 4 * h].rearrange("p t c -> p (t c)"), PB[h][:], ACT.Identity)
            ins.then_inc(sem["qkv_sb"], 1)
            act.wait_ge(sem["qkv"], upto("qkv", i, 4))
            SC.activation(v_tok[:, 0], PB[2][:, 0:C], ACT.Identity).then_inc(sem["qkv_sb"], 1)
            SC.activation(prob[:, 0:P - BACK], ident[:, 0:P - BACK], ACT.Identity, scale=0.0).then_inc(sem["qkv_sb"], 1)
            yield
            yield
            for t in range(1, NT + 2):
                if t <= NT:
                    n = t - 1
                    act.wait_ge(sem["masked"], upto("masked", i, n + 1))
                    if n >= 2:
                        act.wait_ge(sem["probd"], upto("probd", i, n - 1))
                    for w in range(3):
                        ins = SC.activation(ex[n % 2][:, w], sm[n % 2][:, w], ACT.Exp, bias=amax[n % 2][:, w:w + 1],
                                            scale=SCALE, accum_out=asum[n % 2][:, w:w + 1])
                    ins.then_inc(sem["expd"], 1)
                if t >= 2:
                    n = t - 2
                    act.wait_ge(sem["prob_ps"], upto("prob_ps", i, n + 1))
                    if n:
                        act.wait_ge(sem["ctx_ps"], upto("ctx_ps", i, n))
                    SC.activation(prob_t[:], PB[2][:, 0:2 * P], ACT.Identity).then_inc(sem["prob_sb"], 1)
                    act.wait_ge(sem["ctx_ps"], upto("ctx_ps", i, n + 1))
                    SC.activation(ctx_t[:, n * P:(n + 1) * P], PB[3][:, 0:P], ACT.Identity).then_inc(sem["ctx_sb"], 1)
                yield
            for h in range(2):
                act.wait_ge(sem["att_out"], upto("att_out", i, h + 1))
                SC.activation(flat4(t1, h), PB[h][:], ACT.Identity).then_inc(sem["t1"], 1)
            yield

        def dve_att(dve, i, link):
            yield from ln_stats(dve, i, 0, t0, link)
            for _ in range(3):
                yield PIECE

            def masked(t):
                dve.wait_ge(sem["score"], upto("score", i, t + 1))
                if t >= 2:
                    dve.wait_ge(sem["expd"], upto("expd", i, t - 1))
                link(V.tensor_tensor(sm[t % 2][:], PB[t % 2][:, 0:KEYS].unsqueeze(1).to_broadcast([P, 3, KEYS]),
                                     band[:], ALU.add))
                link(V.tensor_reduce(amax[t % 2][:], sm[t % 2][:], AX.X, ALU.max))
                V.tensor_scalar(amax[t % 2][:], amax[t % 2][:], -SCALE, None, ALU.mult).then_inc(sem["masked"], 1)

            masked(0)
            yield PIECE
            for t in range(1, NT + 2):
                if t < NT:
                    masked(t)
                if t <= NT:
                    n = t - 1
                    yield
                    dve.wait_ge(sem["expd"], upto("expd", i, n + 1))
                    if n:
                        dve.wait_ge(sem["probd"], upto("probd", i, n))
                    link(V.reciprocal(arec[:], asum[n % 2][:]))
                    link(V.tensor_scalar(arec[:], arec[:], 1.0 / len(WINDOWS), None, ALU.mult))
                    if n:
                        dve.wait_ge(sem["prob_ps"], upto("prob_ps", i, n))
                    else:
                        dve.wait_ge(sem["qkv_sb"], upto("qkv_sb", i, 5))
                    p, e = prob[:, P - BACK:2 * P], ex[n % 2]
                    link(V.tensor_scalar(p, e[:, 0], arec[:, 0:1], None, ALU.mult))
                    link(V.scalar_tensor_tensor(p, e[:, 1], arec[:, 1:2], p, ALU.mult, ALU.add))
                    V.scalar_tensor_tensor(p, e[:, 2], arec[:, 2:3], p, ALU.mult, ALU.add).then_inc(sem["probd"], 1)
                yield PIECE
            yield PIECE

        def pe_logits(pe, i, n, router):
            pe.wait_ge(sem["ln_utsb"], upto("ln_utsb", i, (4, 6)[n]))
            for t in range(NT):
                ins = T.matmul(PB[2][:, t * E8:(t + 1) * E8], utile(t), router[:], start=True, stop=True)
            ins.then_inc(sem["logit"], 1)

        def act_route(act, i, n):
            act.wait_ge(sem["g_e"], upto("g_e", i, n + 1))
            SC.activation(gp[:], gl[:], ACT.Exp).then_inc(sem["g_exp"], 1)

        def dve_route(dve, i, n, link):
            def ex8(row):
                return gsm[:, row].unsqueeze(2).to_broadcast([P, NT, E8])
            dve.wait_ge(sem["logit"], upto("logit", i, n + 1))
            link(V.tensor_copy(gl[:], PB[2][:, 0:NT * E8].rearrange("p (t e) -> p t e", e=E8)))
            link(V.tensor_reduce(gsm[:, 0], gl[:], AX.X, ALU.max))
            V.tensor_tensor(gl[:], gl[:], ex8(0), ALU.subtract).then_inc(sem["g_e"], 1)
            yield
            dve.wait_ge(sem["g_exp"], upto("g_exp", i, n + 1))
            link(V.tensor_reduce(gsm[:, 1], gp[:], AX.X, ALU.add))
            link(V.reciprocal(gsm[:, 2], gsm[:, 1]))
            link(V.tensor_tensor(gp[:], gp[:], ex8(2), ALU.mult))
            p, revb = gp, rev[:].unsqueeze(1).to_broadcast([P, NT, E8])
            for k, oh in enumerate((oh1, oh2)):
                link(V.tensor_reduce(gsm[:, 3 + k], p[:], AX.X, ALU.max))
                link(V.tensor_tensor(gv[:], p[:], ex8(3 + k), ALU.is_equal))
                link(V.tensor_tensor(gv[:], gv[:], revb, ALU.mult))
                link(V.tensor_reduce(gsm[:, 5], gv[:], AX.X, ALU.max))
                link(V.tensor_tensor(oh[:], gv[:], ex8(5), ALU.is_equal))
                if k == 0:
                    link(V.scalar_tensor_tensor(gq[:], oh1[:], -2.0, gp[:], ALU.mult, ALU.add))
                    p = gq
            link(V.tensor_tensor(gsm[:, 6], gsm[:, 3], gsm[:, 4], ALU.add))
            if n == 0:
                link(V.tensor_scalar(gsm[:, 6], gsm[:, 6], 1e-12, None, ALU.max))
            else:
                link(V.tensor_scalar(gsm[:, 6], gsm[:, 6], 1e-9, None, ALU.add))
            link(V.reciprocal(gsm[:, 7], gsm[:, 6]))
            link(V.tensor_tensor(oh1[:], oh1[:], ex8(3), ALU.mult))
            link(V.tensor_tensor(oh2[:], oh2[:], ex8(4), ALU.mult))
            link(V.tensor_tensor(oh1[:], oh1[:], oh2[:], ALU.add))
            V.tensor_tensor(gates[:], oh1[:], ex8(7), ALU.mult).then_inc(sem["gated"], 1)

        def pe_gate_rows(pe, out, h, e):
            for t in range(4):
                ins = T.matmul(out[:, t * P:(t + 1) * P], gates[:, 4 * h + t, e:e + 1].to_broadcast([P, P]), ident[:],
                               start=True, stop=True)
            return ins

        def sp_e1(sp, i):
            for e in range(E8):
                if e >= 2:
                    sp.wait_ge(sem["y1_ps"], upto("y1_ps", i, 2 * (e - 1)))
                    settle(sp)
                sp.dma_start(e1w[:, e % 2, 0], A["L2_ffn_w1"][e]).then_inc(sem["e1_in%d" % (e % 2)], 16)
                sp.dma_start(e1w[:, e % 2, 1], A["L2_ffn_w2"][e]).then_inc(sem["e1_in%d" % (e % 2)], 16)

        def pe_moe1(pe, i):
            pe.wait_ge(sem["t1"], upto("t1", i))
            pe_ln(pe, i, 1)
            pe_logits(pe, i, 0, router1)
            yield
            pe.wait_ge(sem["gated"], upto("gated", i, 1))
            for h in range(2):
                for t in range(4):
                    ins = T.transpose(PB[h][0:E8, t * P:(t + 1) * P], gates[:, 4 * h + t], ident[:])
                ins.then_inc(sem["gt_ps"], 1)
            pe.wait_ge(sem["gt_sb"], upto("gt_sb", i))
            for h in range(2):
                T.matmul(PB[2 + h][:], ident[:], flat4(t1, h), start=True, stop=False)
                T.matmul(PB[2 + h][:], ident[:], flat4(u, h), start=False, stop=False)
                for t in range(4):
                    n = 4 * h + t
                    T.matmul(PB[2 + h][:, t * P:(t + 1) * P], gates_t[0:E8, n * P:(n + 1) * P], b2[:],
                             start=False, stop=False)
            yield
            for n in range(2 * E8 + 1):
                if n < 2 * E8:
                    e, h = divmod(n, 2)
                    pe.wait_ge(sem["e1_in%d" % (e % 2)], upto("e1_in%d" % (e % 2), i, 32 * (e // 2 + 1)))
                    if n:
                        pe.wait_ge(sem["gelu"], upto("gelu", i, n))
                        pe.wait_ge(sem["gh"], upto("gh", i, n))
                    T.matmul(PB[0][:], e1w[:, e % 2, 0], uhalf(h), start=True, stop=True).then_inc(sem["h_ps"], 1)
                    pe_gate_rows(pe, PB[1], h, e).then_inc(sem["gb_ps"], 1)
                if n:
                    e, h = divmod(n - 1, 2)
                    pe.wait_ge(sem["gh"], upto("gh", i, n))
                    for t in range(4):
                        ins = T.matmul(PB[2 + h][:, t * P:(t + 1) * P], gated_h[:, h, t * P:(t + 1) * P],
                                       e1w[:, e % 2, 1], start=False, stop=(e == E8 - 1 and t == 3))
                    ins.then_inc(sem["y1_ps"], 1)
                yield

        def act_moe1(act, i):
            act_ln(act, i, 1)
            act_route(act, i, 0)
            yield
            for h in range(2):
                act.wait_ge(sem["gt_ps"], upto("gt_ps", i, h + 1))
                SC.activation(gates_t[0:E8, h * HALF:(h + 1) * HALF], PB[h][0:E8, :], ACT.Identity).then_inc(sem["gt_sb"], 1)
            yield
            for n in range(2 * E8):
                e, h = divmod(n, 2)
                act.wait_ge(sem["h_ps"], upto("h_ps", i, n + 1))
                if n >= 2:
                    act.wait_ge(sem["gh"], upto("gh", i, n - 1))
                SC.activation(act_h[:, h], PB[0][:], ACT.Gelu, bias=b1[:, e:e + 1]).then_inc(sem["gelu"], 1)
                yield
            for h in range(2):
                act.wait_ge(sem["y1_ps"], upto("y1_ps", i, 15 + h))
                SC.activation(flat4(t0, h), PB[2 + h][:], ACT.Identity).then_inc(sem["t2"], 1)
            yield

        def dve_moe1(dve, i, link):
            dve.wait_ge(sem["t1"], upto("t1", i))
            yield from ln_stats(dve, i, 1, t1, link)
            yield from dve_route(dve, i, 0, link)
            yield PIECE
            yield PIECE
            for n in range(2 * E8):
                h = n % 2
                dve.wait_ge(sem["gelu"], upto("gelu", i, n + 1))
                dve.wait_ge(sem["gb_ps"], upto("gb_ps", i, n + 1))
                if n >= 2:
                    dve.wait_ge(sem["y1_ps"], upto("y1_ps", i, n - 1))
                V.tensor_tensor(gated_h[:, h], act_h[:, h], PB[1][:], ALU.mult).then_inc(sem["gh"], 1)
                yield PIECE
            yield PIECE

        def heads(ap):
            return ap.rearrange("p (h d) -> p h d", d=HDIM)

        def hb(ap, n=HDIM):
            return ap.unsqueeze(2).to_broadcast([ap.shape[0], HEADS, n])

        def pe_ssm(pe, i):
            pe.wait_ge(sem["xn3"], upto("xn3", i))
            pe.wait_ge(sem["t2"], upto("t2", i))
            for t in range(NT):
                ins = T.transpose(PB[t // 4][:, (t % 4) * P:(t % 4 + 1) * P], t1[:, t], ident[:])
                if t % 4 == 3:
                    ins.then_inc(sem["xn3_ps"], 1)
            yield
            pe.wait_ge(sem["xn3_t"], upto("xn3_t", i))
            for t in range(NT):
                if t >= 2:
                    pe.wait_ge(sem["z_sb"], upto("z_sb", i, t - 1))
                    pe.wait_ge(sem["xbc_sb"], upto("xbc_sb", i, t - 1))
                T.matmul(PB[t % 2][:, 0:ZDT], utile(t), w_zdt[:], start=True, stop=True).then_inc(sem["z_ps"], 1)
                out = PB[2 + t % 2][:, 0:XBC]
                T.matmul(out, ones[0:1, :], cb_row[:], start=True, stop=False)
                for k in range(CONVK):
                    ins = T.matmul(out, u_t[:, t * P + k:t * P + k + P], w_xbc[:, k], start=False, stop=(k == CONVK - 1))
                ins.then_inc(sem["x_ps"], 1)
                yield
            pe.wait_ge(sem["z_sb"], upto("z_sb", i))
            pe.wait_ge(sem["xbc_sb"], upto("xbc_sb", i))
            for n in range(4):
                m, h = divmod(n, 2)
                for k in range(CONVK):
                    ins = T.matmul(PB[n][0:STATE, :], w_xbc[:, k, INNER + m * STATE:INNER + (m + 1) * STATE],
                                   u_t[:, h * HALF + k:h * HALF + k + HALF], start=(k == 0), stop=(k == CONVK - 1))
                ins.then_inc(sem["bc_ps"], 1)
            yield
            pe.wait_ge(sem["la"], upto("la", i))
            pe.wait_ge(sem["bc_sb"], upto("bc_sb", i))
            laf = la[:].rearrange("p t h -> p (t h)")
            n64 = NT * HEADS
            T.matmul(PB[0][:, 0:n64], tri[:], laf, start=True, stop=True)
            T.matmul(PB[0][:, n64:2 * n64], later[:], laf, start=True, stop=True)
            T.matmul(PB[0][:, 2 * n64:3 * n64], ones[:], laf, start=True, stop=True).then_inc(sem["cum"], 1)
            pe.wait_ge(sem["ecum"], upto("ecum", i))

            def seg(c):
                if c:
                    pe.wait_ge(sem["decay"], upto("decay", i, c))
                for h in range(2):
                    T.matmul(PB[h][:], ident[:], future[:].unsqueeze(1).to_broadcast([P, 4, P]), start=True, stop=False)
                    T.matmul(PB[h][:], ntri[:], la[:, c, 4 * h:4 * h + 4].unsqueeze(2).to_broadcast([P, 4, P]),
                             start=False, stop=False)
                    for k in range(4):
                        n = 4 * h + k
                        ins = T.matmul(PB[h][:, k * P:(k + 1) * P], la[:, c, n:n + 1].to_broadcast([P, P]), tri[:],
                                       start=False, stop=(k == 3))
                ins.then_inc(sem["seg"], 1)

            seg(0)
            yield
            for c in range(NT):
                if c:
                    pe.wait_ge(sem["state"], upto("state", i, c))
                T.matmul(PB[2][:, 0:P], b_t[0:STATE, c * P:(c + 1) * P], c_t[0:STATE, c * P:(c + 1) * P],
                              start=True, stop=True).then_inc(sem["cbt"], 1)
                if c + 1 < NT:
                    seg(c + 1)
                pe.wait_ge(sem["mix"], upto("mix", i, c + 1))
                pe.wait_ge(sem["xdr"], upto("xdr", i, c + 1))
                T.matmul(PB[2][0:STATE, 0:INNER], xbc[:, c, INNER:INNER + STATE], xdr[:], start=True, stop=True).then_inc(sem["ds_ps"], 1)
                if c:
                    pe.wait_ge(sem["y_sb"], upto("y_sb", i, c))
                for h in range(HEADS):
                    T.matmul(PB[3][:, h * HDIM:(h + 1) * HDIM], mix[:, h], xdt[:, h * HDIM:(h + 1) * HDIM],
                             start=True, stop=True)
                T.matmul(PB[3][:, INNER:2 * INNER], c_t[0:STATE, c * P:(c + 1) * P], state[:],
                              start=True, stop=True).then_inc(sem["y_ps"], 1)
                yield
            pe.wait_ge(sem["yn"], upto("yn", i))
            pe.wait_ge(sem["state"], upto("state", i))
            pe.wait_ge(sem["y_sb"], upto("y_sb", i))
            for n in range(4):
                a, h = divmod(n, 2)
                for t in range(4):
                    ins = T.transpose(PB[n][:, t * P:(t + 1) * P], ys[:, 4 * h + t, a * P:(a + 1) * P], ident[:])
                ins.then_inc(sem["yt_ps"], 1)
            yield
            pe.wait_ge(sem["yt_sb"], upto("yt_sb", i))
            for h in range(2):
                for t in range(4):
                    n = 4 * h + t
                    for a in range(2):
                        ins = T.matmul(PB[h][:, t * P:(t + 1) * P], y_t[:, a, n * P:(n + 1) * P], w_out[:, a],
                                       start=(a == 0), stop=(a == 1))
                ins.then_inc(sem["o_ps"], 1)
            yield

        def act_ssm(act, i):
            act_ln(act, i, 2, transposed=False)
            act.wait_ge(sem["rms_sq"], upto("rms_sq", i, 1))
            SC.activation(rms[:, 1], rms[:, 0], ACT.Sqrt, scale=1.0 / C, bias=eps_rms1[:, 0:1]).then_inc(sem["rms_std"], 1)
            for h in range(2):
                act.wait_ge(sem["xn3_ps"], upto("xn3_ps", i, h + 1))
                SC.activation(uhalf(h), PB[h][:], ACT.Identity, scale=rms_w[:, 0:1]).then_inc(sem["xn3_t"], 1)
            yield
            for t in range(NT):
                act.wait_ge(sem["z_ps"], upto("z_ps", i, t + 1))
                SC.activation(zs[:, t], PB[t % 2][:, 0:INNER], ACT.Silu)
                SC.activation(dtr[:, t], PB[t % 2][:, INNER:ZDT], ACT.Identity).then_inc(sem["z_sb"], 1)
                act.wait_ge(sem["x_ps"], upto("x_ps", i, t + 1))
                SC.activation(xbc[:, t], PB[2 + t % 2][:, 0:XBC], ACT.Silu).then_inc(sem["xbc_sb"], 1)
                yield
            for n in range(4):
                m, h = divmod(n, 2)
                act.wait_ge(sem["bc_ps"], upto("bc_ps", i, n + 1))
                SC.activation((b_t, c_t)[m][0:STATE, h * HALF:(h + 1) * HALF], PB[n][0:STATE, :], ACT.Silu,
                                   bias=cb_col[:, m:m + 1]).then_inc(sem["bc_sb"], 1)
            yield
            act.wait_ge(sem["dt_abs"], upto("dt_abs", i))
            SC.activation(dtx[:, 2], dtx[:, 1], ACT.Exp, scale=-1.0).then_inc(sem["dt_exp"], 1)
            act.wait_ge(sem["dt_w"], upto("dt_w", i))
            SC.activation(dtx[:, 4], dtx[:, 3], ACT.Ln).then_inc(sem["dt_ln"], 1)
            act.wait_ge(sem["cum"], upto("cum", i))
            SC.activation(ecum[:].rearrange("p a b -> p (a b)"), PB[0][:, 0:3 * NT * HEADS], ACT.Exp).then_inc(sem["ecum"], 1)
            yield
            for c in range(NT):
                act.wait_ge(sem["seg"], upto("seg", i, c + 1))
                if c:
                    act.wait_ge(sem["mix"], upto("mix", i, c))
                for h in range(2):
                    ins = SC.activation(decay[:, 4 * h:4 * h + 4].rearrange("p h i -> p (h i)"), PB[h][:], ACT.Exp)
                ins.then_inc(sem["decay"], 1)
                yield
            act.wait_ge(sem["rms_sq"], upto("rms_sq", i, 2))
            SC.activation(rms[:, 1], rms[:, 0], ACT.Sqrt, scale=1.0 / INNER, bias=eps_ln[:, 0:1]).then_inc(sem["rms_std"], 1)
            for n in range(4):
                a, h = divmod(n, 2)
                act.wait_ge(sem["yt_ps"], upto("yt_ps", i, n + 1))
                SC.activation(y_t[:, a, h * HALF:(h + 1) * HALF], PB[n][:], ACT.Identity, scale=gnorm[:, a:a + 1]).then_inc(sem["yt_sb"], 1)
            yield
            yield

        def dve_ssm(dve, i, link):
            n64 = NT * HEADS
            dve.wait_ge(sem["t2"], upto("t2", i))
            yield from ln_stats(dve, i, 2, t0, link)
            dve.wait_ge(sem["ln_u"], upto("ln_u", i, 3))
            link(V.tensor_tensor(t1[:], u[:], u[:], ALU.mult))
            V.tensor_reduce(rms[:, 0], t1[:], AX.X, ALU.add).then_inc(sem["rms_sq"], 1)
            dve.wait_ge(sem["rms_std"], upto("rms_std", i, 1))
            link(V.reciprocal(rms[:, 2], rms[:, 1]))
            for t in range(NT):
                ins = V.tensor_scalar(t1[:, t], u[:, t], rms[:, 2, t:t + 1], None, ALU.mult)
            ins.then_inc(sem["xn3"], 1)
            yield PIECE
            for _ in range(NT):
                yield PIECE
            link(V.tensor_tensor(t0[:], t0[:], u[:], ALU.add))
            dve.wait_ge(sem["z_sb"], upto("z_sb", i))
            dt3 = dtx[:, 0].rearrange("p (t h) -> p t h", h=HEADS)
            link(V.tensor_tensor(dt3, dtr[:], dt_bias[:].unsqueeze(1).to_broadcast([P, NT, HEADS]), ALU.add))
            V.scalar_tensor_tensor(dtx[:, 1], dtx[:, 0], -1.0, dtx[:, 0], ALU.mult, ALU.max).then_inc(sem["dt_abs"], 1)
            yield PIECE
            dve.wait_ge(sem["dt_exp"], upto("dt_exp", i))
            V.tensor_scalar(dtx[:, 3], dtx[:, 2], 1.0, None, ALU.add).then_inc(sem["dt_w"], 1)
            yield
            dve.wait_ge(sem["dt_ln"], upto("dt_ln", i))
            link(V.tensor_scalar(dtx[:, 3], dtx[:, 3], -1.0, None, ALU.add))
            link(V.tensor_scalar(dtx[:, 5], dtx[:, 3], 0.0, None, ALU.is_equal))
            link(V.tensor_tensor(dtx[:, 4], dtx[:, 4], dtx[:, 5], ALU.add))
            link(V.tensor_tensor(dtx[:, 3], dtx[:, 3], dtx[:, 5], ALU.add))
            link(V.reciprocal(dtx[:, 3], dtx[:, 3]))
            link(V.tensor_tensor(dtx[:, 4], dtx[:, 4], dtx[:, 3], ALU.mult))
            link(V.tensor_tensor(dtx[:, 4], dtx[:, 4], dtx[:, 2], ALU.mult))
            link(V.scalar_tensor_tensor(dtx[:, 0], dtx[:, 0], 0.0, dtx[:, 4], ALU.max, ALU.add))
            V.tensor_tensor(la[:], dt3, neg_a[:].unsqueeze(1).to_broadcast([P, NT, HEADS]), ALU.mult).then_inc(sem["la"], 1)
            dve.wait_ge(sem["xbc_sb"], upto("xbc_sb", i))
            for t in range(NT):
                ins = V.tensor_tensor(heads(ys[:, t]), heads(xbc[:, t, 0:INNER]), hb(dskip[:]), ALU.mult)
            link(ins)
            link(V.memset(state[:], 0.0))
            yield PIECE
            dve.wait_ge(sem["ecum"], upto("ecum", i))
            ec = ecum[:].rearrange("p a (t h) -> p a t h", h=HEADS)
            for c in range(NT):
                if c:
                    dve.wait_ge(sem["ds_ps"], upto("ds_ps", i, c))
                    dve.wait_ge(sem["y_ps"], upto("y_ps", i, c))
                link(V.tensor_tensor(heads(xdt[:]), heads(xbc[:, c, 0:INNER]), hb(dt3[:, c]), ALU.mult))
                V.tensor_tensor(heads(xdr[:]), heads(xdt[:]), hb(ec[:, 1, c]), ALU.mult).then_inc(sem["xdr"], 1)
                dve.wait_ge(sem["decay"], upto("decay", i, c + 1))
                dve.wait_ge(sem["cbt"], upto("cbt", i, c + 1))
                V.tensor_tensor(mix[:], decay[:], PB[2][:, 0:P].unsqueeze(1).to_broadcast([P, HEADS, P]),
                                     ALU.mult).then_inc(sem["mix"], 1)
                yield
                dve.wait_ge(sem["y_ps"], upto("y_ps", i, c + 1))
                link(V.tensor_tensor(ys[:, c], ys[:, c], PB[3][:, 0:INNER], ALU.add))
                link(V.tensor_tensor(heads(yoff[:]), heads(PB[3][:, INNER:2 * INNER]), hb(ec[:, 0, c]), ALU.mult))
                V.tensor_tensor(ys[:, c], ys[:, c], yoff[:], ALU.add).then_inc(sem["y_sb"], 1)
                dve.wait_ge(sem["ds_ps"], upto("ds_ps", i, c + 1))
                link(V.tensor_tensor(heads(state[:]), heads(state[:]), hb(ec[0:STATE, 2, c]), ALU.mult))
                V.tensor_tensor(state[:], state[:], PB[2][0:STATE, 0:INNER], ALU.add).then_inc(sem["state"], 1)
                dve.wait_ge(sem["state"], upto("state", i, c + 1))
                yield PIECE
            dve.wait_ge(sem["y_sb"], upto("y_sb", i))
            link(V.tensor_tensor(ys[:], ys[:], zs[:], ALU.mult), "yn")
            link(V.tensor_tensor(zs[:], ys[:], ys[:], ALU.mult))
            link(V.tensor_reduce(rms[:, 0], zs[:], AX.X, ALU.add), "rms_sq")
            yield PIECE
            dve.wait_ge(sem["rms_std"], upto("rms_std", i, 2))
            link(V.reciprocal(rms[:, 2], rms[:, 1]))
            for t in range(NT):
                dve.wait_ge(sem["o_ps"], upto("o_ps", i, t // 4 + 1))
                ins = V.scalar_tensor_tensor(t1[:, t], PB[t // 4][:, (t % 4) * P:(t % 4 + 1) * P], rms[:, 2, t:t + 1],
                                             t0[:, t], ALU.mult, ALU.add)
            ins.then_inc(sem["t3"], 1)
            dve.wait_ge(sem["t3"], upto("t3", i))
            yield PIECE

        W3, W2 = HID, 2 * HID

        def sp_e2(sp, i):
            for e in range(E8):
                if e >= 2:
                    sp.wait_ge(sem["y2_ps"], upto("y2_ps", i, 6 * (e - 1)))
                    settle(sp)
                s = "e2_in%d" % (e % 2)
                sp.dma_start(e2w[:, e % 2, 0:HID], A["moe2_w1_t"][e]).then_inc(sem[s], 16)
                sp.dma_start(e2w[:, e % 2, W3:W3 + HID], A["moe2_w3_t"][e]).then_inc(sem[s], 16)
                for k, m in enumerate(HTILES):
                    sp.dma_start(e2w[0:m, e % 2, W2 + k * C:W2 + (k + 1) * C],
                                      A["moe2_w2_t"][e, k * P:k * P + m]).then_inc(sem[s], 16)

        def pe_moe2(pe, i):
            pe_ln(pe, i, 3)
            pe_logits(pe, i, 1, router2)
            yield
            pe.wait_ge(sem["gated"], upto("gated", i, 2))
            for h in range(2):
                T.matmul(PB[2 + h][:], ident[:], flat4(t1, h), start=True, stop=False)

            def y_part(n):
                eh, k = divmod(n, 3)
                e, h = divmod(eh, 2)
                m = HTILES[k]
                pe.wait_ge(sem["hh"], upto("hh", i, n + 1))
                for t in range(4):
                    ins = T.matmul(PB[2 + h][:, t * P:(t + 1) * P], gated_h[0:m, n % 2, t * P:(t + 1) * P],
                                   e2w[0:m, e % 2, W2 + k * C:W2 + (k + 1) * C], start=False,
                                   stop=(e == E8 - 1 and k == 2 and t == 3))
                ins.then_inc(sem["y2_ps"], 1)

            for n in range(48):
                eh, k = divmod(n, 3)
                e, h = divmod(eh, 2)
                m = HTILES[k]
                if k == 0:
                    pe.wait_ge(sem["e2_in%d" % (e % 2)], upto("e2_in%d" % (e % 2), i, 80 * (e // 2 + 1)))
                    if n:
                        pe.wait_ge(sem["hh"], upto("hh", i, n))
                    pe_gate_rows(pe, PB[1], h, e).then_inc(sem["gb2"], 1)
                if n:
                    pe.wait_ge(sem["silu"], upto("silu", i, n))
                T.matmul(PB[0][0:m, :], e2w[:, e % 2, k * P:k * P + m], uhalf(h), start=True, stop=True).then_inc(sem["h1_ps"], 1)
                if k == 0:
                    pe.wait_ge(sem["gu"], upto("gu", i, eh + 1))
                else:
                    pe.wait_ge(sem["hh"], upto("hh", i, n))
                T.matmul(PB[1][0:m, :], e2w[:, e % 2, W3 + k * P:W3 + k * P + m], gated_u[:, eh % 2],
                              start=True, stop=True).then_inc(sem["h3_ps"], 1)
                if n:
                    y_part(n - 1)
                yield
            y_part(47)
            yield

        def act_moe2(act, i):
            act_ln(act, i, 3)
            act_route(act, i, 1)
            yield
            for n in range(48):
                m = HTILES[n % 3]
                act.wait_ge(sem["h1_ps"], upto("h1_ps", i, n + 1))
                if n >= 2:
                    act.wait_ge(sem["hh"], upto("hh", i, n - 1))
                SC.activation(act_h[0:m, n % 2], PB[0][0:m, :], ACT.Silu).then_inc(sem["silu"], 1)
                yield
            for h in range(2):
                act.wait_ge(sem["y2_ps"], upto("y2_ps", i, 45 + 3 * h))
                SC.activation(flat4(t0, h), PB[2 + h][:], ACT.Identity).then_inc(sem["out_sb"], 1)
            yield

        def dve_moe2(dve, i, link):
            yield from ln_stats(dve, i, 3, t1, link)
            yield from dve_route(dve, i, 1, link)
            yield PIECE
            for n in range(48):
                eh, k = divmod(n, 3)
                h = eh % 2
                m = HTILES[k]
                if k == 0:
                    dve.wait_ge(sem["gb2"], upto("gb2", i, eh + 1))
                    if eh >= 2:
                        dve.wait_ge(sem["h3_ps"], upto("h3_ps", i, 3 * (eh - 1)))
                    V.tensor_tensor(gated_u[:, eh % 2], uhalf(h), PB[1][:], ALU.mult).then_inc(sem["gu"], 1)
                dve.wait_ge(sem["silu"], upto("silu", i, n + 1))
                dve.wait_ge(sem["h3_ps"], upto("h3_ps", i, n + 1))
                if n >= 2:
                    dve.wait_ge(sem["y2_ps"], upto("y2_ps", i, n - 1))
                V.tensor_tensor(gated_h[0:m, n % 2], act_h[0:m, n % 2], PB[1][0:m, :], ALU.mult).then_inc(sem["hh"], 1)
                yield PIECE
            yield PIECE

        def sp_out(sp, i):
            sp.wait_ge(sem["out_sb"], upto("out_sb", i))
            settle(sp)
            sp.dma_start(A["out"][bass.ds(i, 1)].rearrange("a (t r) w c -> (a r w) t c", t=NT), t0[:]).then_inc(sem["out"], 16)

        SECOND = ([6, 4, 6] + [3] * 10 + [8] + [8, 8] + [3] * 17 + [8] + [3] * 8 + [14, 6] + [8] * 8 + [6, 5]
                  + [8] + [3.6] * 49)
        FIRST = [10, 14] + [6] * NG + [10] + [3] * SORT_T

        def order():
            out, a, b, ta, tb = [], 0, 0, 0.0, 0.0
            while a < len(FIRST) or b < len(SECOND):
                fa = (ta + FIRST[a] / 2) / sum(FIRST) if a < len(FIRST) else 9
                fb = (tb + SECOND[b] / 2) / sum(SECOND) if b < len(SECOND) else 9
                if fa < fb:
                    ta, a = ta + FIRST[a], a + 1
                    out.append(("first", (ta + tb) / (sum(FIRST) + sum(SECOND))))
                else:
                    tb, b = tb + SECOND[b], b + 1
                    out.append(("second", (ta + tb) / (sum(FIRST) + sum(SECOND))))
            return out

        def interleave(first, second):
            for part, _ in order():
                gen = first if part == "first" else second
                if gen is not None:
                    next(gen)
            for gen in (first, second):
                assert gen is None or next(gen, None) is None and next(gen, "end") == "end"

        def pe_second(pe, i):
            yield from pe_att(pe, i)
            yield from pe_moe1(pe, i)
            yield from pe_ssm(pe, i)
            yield from pe_moe2(pe, i)

        def pe_first(pe, i):
            yield from pe_pre(pe, i)
            yield from pe_corr(pe, i, 0)

        def act_second(act, i):
            yield from act_att(act, i)
            yield from act_moe1(act, i)
            yield from act_ssm(act, i)
            yield from act_moe2(act, i)

        def act_first(act, i):
            yield from act_pre(act, i)
            yield from act_corr(act, i, 0)

        def dve_second(dve, i):
            dve.wait_ge(sem["out"], upto("out", i, 16))
            link = Chain(dve, "dve_post", i)
            dve.wait_ge(sem["ranked"], upto("ranked", i))
            link(V.tensor_copy(t0[:], x2_tok[:]), "t_in")
            yield from dve_att(dve, i, link)
            yield from dve_moe1(dve, i, link)
            yield from dve_ssm(dve, i, link)
            yield from dve_moe2(dve, i, link)
            link.end()

        def dve_sorts(dve, i):
            link = Chain(dve, "dve_sort", i)
            for h in range(2):
                yield from dve_sort(dve, i, h, link)
            link.end()

        SORT_STEPS = 2 * 55

        def dve_body(dve, i, first, sort, second):
            gens = dict(first=dve_pre(dve, i + 1) if first else None, second=dve_second(dve, i - 1) if second else None)
            sorts, steps = (dve_sorts(dve, i), 0) if sort else (None, 0)

            def step():
                nonlocal steps
                if sorts is not None and steps < SORT_STEPS:
                    next(sorts)
                    steps += 1

            if sort:
                step()
            for part, share in order():
                gen = gens[part]
                while gen is not None and next(gen) is not PIECE:
                    step()
                while sort and steps < min(share, 1) * SORT_STEPS:
                    step()
            if sort:
                assert next(sorts, "end") == "end" and steps == SORT_STEPS
            for gen in gens.values():
                assert gen is None or next(gen, "end") == "end"

        def whole(gen):
            for _ in gen:
                pass

        bodies = [0]

        def run(eng, body):
            body(-1, True, False, False)
            body(0, True, True, False)
            if IMGS > 2:
                with eng.Fori(1, IMGS - 1) as i:
                    body(i, True, True, True)
            body(IMGS - 1, False, True, True)
            body(IMGS, False, False, True)

        block = ctx.enter_context(nc.Block())

        @block.sync
        def _(sp):
            sp_load(sp)
            sp_zero_quads(sp)
            others_prep(sp)
            sp.sem_inc(sem["out"], 16)

            def body(i, first, sort, second):
                if first:
                    sp_pre(sp, i + 1)
                if second:
                    sp_e1(sp, i - 1)
                    sp_e2(sp, i - 1)
                    sp_out(sp, i - 1)

            run(sp, body)
            sp.wait_ge(sem["out"], 16 * (IMGS + 1))

        @block.scalar
        def _(act):
            act_prep(act)

            def body(i, first, sort, second):
                if sort:
                    act.wait_ge(sem["t_in"], upto("t_in", i, 0))
                    SC.activation(x2_tok[:], x1_tok[:], ACT.Identity).then_inc(sem["x2_copy"], 1)
                    whole(act_corr(act, i, 1))
                interleave(act_first(act, i + 1) if first else None, act_second(act, i - 1) if second else None)

            run(act, body)

        @block.vector
        def _(dve):
            dve_prep(dve)
            run(dve, lambda i, first, sort, second: dve_body(dve, i, first, sort, second))

        @block.gpsimd
        def _(pool):
            others_prep(pool)

            def body(i, first, sort, second):
                if first:
                    whole(pool_pre(pool, i + 1))

            run(pool, body)

        @block.tensor
        def _(pe):
            others_prep(pe)

            def body(i, first, sort, second):
                if sort:
                    whole(pe_corr(pe, i, 1))
                interleave(pe_first(pe, i + 1) if first else None, pe_second(pe, i - 1) if second else None)

            run(pe, body)



CHAIN_N = dict(dve_pre=19, dve_post=159, dve_sort=112)


def constants():
    k, j = np.arange(P)[:, None], np.arange(P)[None, :]
    f = np.float32
    key, q = np.arange(KEYS)[None, :], np.arange(P)[:, None] + BACK
    band = np.stack([np.where((key <= q) & (key > q - w), 0.0, NEG) for w in WINDOWS], 1)
    tok = np.arange(TOK).reshape(NT, P).T[:, :, None]
    tap = np.arange(TAPS)[None, None, :]
    ys, xs = tok // WIDTH + tap // 3, tok % WIDTH + tap % 3
    return dict(
        c_ident=np.eye(P, dtype=f), c_gavg=((k // GROUP == j // GROUP) / GROUP).astype(f),
        c_tri=(k <= j).astype(f), c_ntri=-(k <= j).astype(f), c_later=(k > j).astype(f),
        c_future=np.where(j < k, NEG, 0.0).astype(f), c_band=band.astype(f),
        c_base=np.stack([ys.reshape(P, -1), xs.reshape(P, -1)], 1).astype(f),
        c_rev=np.broadcast_to(E8 - np.arange(E8), (P, E8)).astype(f),
    )


def layouts(a):
    t = np.ascontiguousarray
    w_in = a["L3_attn_W_in"]
    conv_b = a["L3_attn_conv_b"]
    out = {n: t(a[n]) for n in (
        "x", "L0_conv_om_kernel", "L0_conv_om_bias", "L0_conv_kernel", "L0_conv_bias", "L2_attn_Wq", "L2_attn_bq",
        "L2_attn_Wk", "L2_attn_bk", "L2_attn_Wv", "L2_attn_bv", "L2_attn_Wo", "L2_attn_bo", "L2_ffn_w1", "L2_ffn_w2",
        "L2_ffn_b2", "L3_attn_conv_b", "L3_attn_dt_bias", "L3_attn_A_log", "L3_attn_Dp", "L3_attn_norm_w")}
    out.update(
        router1_t=t(a["L2_ffn_router_w"].T), router2_t=t(a["L3_ffn_router_w"].T), b1_t=t(a["L2_ffn_b1"].T),
        w_zdt_t=t(np.concatenate([w_in[:INNER], w_in[INNER + XBC:]]).T), w_xbc_t=t(w_in[INNER:INNER + XBC].T),
        conv_w_t=t(a["L3_attn_conv_w"].T), cb_bc=t(conv_b[INNER:].reshape(2, STATE).T),
        gnorm_t=t(a["L3_attn_gnorm_w"].reshape(2, P).T),
        w_out_t=t(a["L3_attn_W_out"].T.reshape(2, P, C).transpose(1, 0, 2)),
        moe2_w1_t=t(a["L3_ffn_w1"].transpose(0, 2, 1)), moe2_w3_t=t(a["L3_ffn_w3"].transpose(0, 2, 1)),
        moe2_w2_t=t(a["L3_ffn_w2"].transpose(0, 2, 1)),
    )
    return out


def kernel(**inputs):
    import concourse.bacc as _bacc
    from concourse.bass_utils import run_bass_kernel_spmd as _run

    arrays = {**constants(), **layouts({n: np.asarray(v) for n, v in inputs.items()})}
    nc = _bacc.Bacc("TRN2", target_bir_lowering=False, num_devices=1)
    A = {n: nc.dram_tensor(n, a.shape, mybir.dt.from_np(a.dtype), kind="ExternalInput").ap()
         for n, a in arrays.items()}
    A["out"] = nc.dram_tensor("out", (IMAGES, HEIGHT, WIDTH, C), mybir.dt.float32, kind="ExternalOutput").ap()
    build(nc, A)
    r = _run(nc, [arrays], core_ids=[0])
    return r.results[0]["out"]
```

```python
import math
from contextlib import ExitStack

import numpy as np

import concourse.bass as bass
from concourse import mybir

IMAGES, HEIGHT, WIDTH, C = 8, 32, 32, 128
P = 128
TOK = HEIGHT * WIDTH
NT = TOK // P
ROWS = P // WIDTH
TAPS = 9
OM = 3 * TAPS
GROUP = 4
PADH = HEIGHT + 2
CELL = WIDTH + 2
QUAD = 4 * C
TG = 3
NG = NT * TAPS // TG
BACK = 32
KEYS = BACK + P
WINDOWS = (4, 16, 32)
E8 = 8
HEADS, HDIM, STATE = 8, 32, 32
INNER = HEADS * HDIM
XBC = INNER + 2 * STATE
CONVK = 4
ZDT = INNER + HEADS
HID = 341
HTILES = (128, 128, HID - 256)
HALF = 512
SORT_T = 4
RANKS = [int(r) for r in np.round(np.linspace(1.0, TOK - 1, C))]
GN_EPS, LN_EPS, RMS1_EPS, RMS2_EPS = 1e-5, 1e-5, float(np.finfo(np.float32).eps), 1e-5
NEG = -1e30
PIECE = "piece"
GAP = dict(att=1, gate=0, dt=1, logit=2, rms=2)
SLOTS = 8
H3_SLOTS = 6
LAG1, LAG2 = 3, 5


def rank_pieces():
    pieces = []
    for c, r in enumerate(RANKS):
        if pieces and r == pieces[-1][2] + 8 * pieces[-1][1]:
            pieces[-1][1] += 1
        else:
            pieces.append([c, 1, r])
    return pieces


def build(nc, A, IMGS=IMAGES, debug=None):
    F32, BF16, I32, U32 = mybir.dt.float32, mybir.dt.bfloat16, mybir.dt.int32, mybir.dt.uint32
    ALU, ACT, AX = mybir.AluOpType, mybir.ActivationFunctionType, mybir.AxisListType
    ctx = ExitStack()
    with ctx:
        def sb(name, shape, dt=F32):
            return ctx.enter_context(nc.sbuf_tensor(name, shape, dt))

        ident = sb("ident", [P, P])
        gavg = sb("gavg", [P, P])
        tri = sb("tri", [P, P])
        later = sb("later", [P, P])
        ident_h = sb("ident_h", [P, P], BF16)
        future_h = sb("future_h", [P, P], BF16)
        ones = sb("ones", [P, P])
        band = sb("band", [P, len(WINDOWS), KEYS])
        base = sb("base", [P, 2, NT * TAPS])
        rev = sb("rev", [P, E8])
        eps_ln = sb("eps_ln", [P, 1])
        eps_rms1 = sb("eps_rms1", [P, 1])
        one_col = sb("one_col", [P, 1])
        om_w = sb("om_w", [P, TAPS, OM])
        om_b = sb("om_b", [1, OM])
        conv_w = sb("conv_w", [P, TAPS, C])
        conv_bias = sb("conv_bias", [1, C])
        wqkvo = sb("wqkvo", [P, 4, C])
        bqk = sb("bqk", [P, 2])
        bv_row = sb("bv_row", [1, C])
        bo_row = sb("bo_row", [1, C])
        router1 = sb("router1", [P, E8])
        router2 = sb("router2", [P, E8])
        b1 = sb("b1", [P, E8])
        b2 = sb("b2", [E8, C])
        w_zdt = sb("w_zdt", [P, ZDT])
        w_xbc = sb("w_xbc", [P, CONVK, XBC])
        cb_row = sb("cb_row", [1, XBC])
        dt_bias = sb("dt_bias", [P, HEADS])
        neg_a = sb("neg_a", [P, HEADS])
        dskip = sb("dskip", [P, HEADS])
        gnorm = sb("gnorm", [P, 2])
        rms_w = sb("rms_w", [P, 1])
        w_out = sb("w_out", [P, 2, C])
        e1w = sb("e1w", [P, 3, 2, C])
        e2w = sb("e2w", [P, 2, 2 * HID + 3 * C])
        x_tok = sb("x_tok", [P, NT, C])
        xn_pad = sb("xn_pad", [P, 3, PADH, WIDTH])
        xn_tok = sb("xn_tok", [P, NT, C])
        x1_tok = xn_tok
        bst = sb("bst", [P, 2, 6])
        mv = sb("mv", [P, 8])
        oms = sb("oms", [P, NT, OM])
        mask = sb("mask", [P, NT, TAPS])
        idx = sb("idx", [P, NT * TAPS], U32)
        w4 = sb("w4", [P, NT * TAPS, 4])
        gath = sb("gath", [P, 2, TG, QUAD])
        diag = sb("diag", [P, 2, TG * 4, P])
        cols = sb("cols", [P, TAPS, P])
        colf = cols[:].rearrange("p k c -> p (k c)")
        n2 = 2 * NT * TAPS

        def pair(at):
            return colf[:, at * n2:(at + 1) * n2].rearrange("p (d n) -> p d n", d=2)

        pos, posi, cell, gt, wym = pair(0), pair(1).bitcast(I32), pair(2), pair(3), pair(4)
        frac = colf[:, 5 * n2:7 * n2].rearrange("p (s d n) -> p s d n", s=2, d=2)
        yn_t = sb("yn_t", [P, TOK])
        corr = sb("corr", [P, SORT_T, TOK])
        srt_a = sb("srt_a", [P, SORT_T, TOK])
        srt_b = sb("srt_b", [P, SORT_T, TOK])
        x2_tok = sb("x2_tok", [P, NT, C])
        t0 = sb("t0", [P, NT, C])
        t1 = sb("t1", [P, NT, C])
        u = sb("u", [P, NT, C])
        u_t = sb("u_t", [P, TOK + CONVK - 1])
        lnst = sb("lnst", [P, NT, 6])
        lnmv = sb("lnmv", [P, NT, 2])
        lnsd = sb("lnsd", [P, 2, NT])
        arena = sb("arena", [P, 10752])
        used = [0]

        def carve(n, *dims):
            a = arena[:, used[0]:used[0] + n]
            used[0] += n
            assert used[0] <= 10752, used
            if len(dims) == 2:
                return a.rearrange("p (a b) -> p a b", b=dims[1])
            if len(dims) == 3:
                return a.rearrange("p (a b c) -> p a b c", b=dims[1], c=dims[2])
            return a

        q_t = carve(TOK)
        k_t = carve(BACK + TOK)
        v_tok = carve((NT + 1) * C, NT + 1, C)
        ctx_t = carve(TOK)
        sm = [carve(3 * KEYS, 3, KEYS) for _ in range(2)]
        ex = [carve(3 * KEYS, 3, KEYS) for _ in range(2)]
        prob = carve(2 * P)
        prob_t = carve(2 * P)
        nmax = [carve(3) for _ in range(2)]
        asum = [carve(3) for _ in range(2)]
        arec = carve(3)
        used[0] = 0
        gl = carve(NT * E8, NT, E8)
        gp = carve(NT * E8, NT, E8)
        gq = carve(NT * E8, NT, E8)
        gv = carve(NT * E8, NT, E8)
        oh1 = carve(NT * E8, NT, E8)
        oh2 = carve(NT * E8, NT, E8)
        gates = carve(NT * E8, NT, E8)
        gsm = carve(8 * NT, 8, NT)
        gates_t = carve(TOK)
        act_h = carve(SLOTS * HALF, SLOTS, HALF)
        gated_h = act_h
        h3_s = carve(H3_SLOTS * HALF, H3_SLOTS, HALF)
        gated_u = carve(2 * HALF, 2, HALF)
        gate_diag = carve(2 * HALF, 2, HALF)
        used[0] = 0
        xbc = carve(NT * XBC, NT, XBC)
        zs = carve(NT * INNER, NT, INNER)
        ys = carve(NT * INNER, NT, INNER)
        b_t = carve(TOK)
        c_t = carve(TOK)
        decay = carve(HEADS * P, HEADS, P)
        mix = carve(HEADS * P, HEADS, P)
        dtr = sb("dtr", [P, NT, HEADS])
        dtx = sb("dtx", [P, 6, NT * HEADS])
        la = sb("la", [P, NT, HEADS])
        ecum = sb("ecum", [P, 3, NT * HEADS])
        xdt, xdr, yoff, state = (u[0:n, 2 * k:2 * k + 2].rearrange("p a c -> p (a c)")
                                 for k, n in enumerate((P, P, P, STATE)))
        rms = sb("rms", [P, 4, NT])
        y_t = arena[:, 0:2 * TOK].rearrange("p (a n) -> p a n", a=2)

        bank = [ctx.enter_context(nc.psum_tensor(f"bank{i}", [P, HALF], F32)) for i in range(8)]
        PA, PB = bank[0:3], bank[3:8]
        GB = (PB[1], PB[4])
        quads = nc.dram_tensor("quads", [CELL * CELL, QUAD], F32, kind="Internal").ap()

        PER = dict(
            x_in=16, x_t=2, gn_mom=4, gn_avg=4, gn_std=2, gn_scale=2, gn_out=2, om_done=1, om_sb=1, sig=1,
            xn_back=2, xn_tok=2, quad_out=16 * 32, idx=1, w4=1, gath0=16 * TG * NG // 2, gath1=16 * TG * NG // 2,
            diag=NG, colt=NG, cols=NG, conv=NT, x1=NT, corr_mm=NT, corr_sb=2 * NT, corr_used=2, x2_copy=1, ranked=2,
            t_in=1, ln_v=4, ln_std=4, ln_u=4, ln_ut=6, ln_utsb=6,
            qkv=4, qkv_sb=5, score=NT, masked=NT, expd=NT, probd=NT, prob_ps=NT, prob_sb=NT, ctx_ps=NT, ctx_sb=NT,
            att_out=2, t1=2, e1_in0=96, e1_in1=96, e1_in2=64, logit=2, g_e=2, g_exp=2, gated=2, gt_ps=2, gt_sb=2,
            h_ps=16, gb_ps=16, gelu=16, gh=16, y1_ps=16, t2=2,
            rms_sq=2, rms_r=1, rms_std=2, xn3=1, xn3_ps=2, xn3_t=2, z_ps=NT, z_sb=NT, x_ps=NT, xbc_sb=NT, bc_ps=4, bc_sb=4,
            dt_abs=1, dt_exp=1, dt_w=1, dt_ln=1, la=1, cum=1, ecum=1, seg=NT, decay=NT, cbt=NT, mix=NT,
            xdr=NT, steps=NT, y_ps=NT, ds_ps=NT, y_sb=NT, state=NT, yn=1, yt_ps=4, yt_sb=4, o_ps=2, t3=1,
            e2_in0=16 * 5 * E8 // 2, e2_in1=16 * 5 * E8 // 2, gb2=16, gate_diag=16, gu=16, h1_ps=48, h3_ps=48, h3_sb=48, silu=48, hh=48, y2_ps=48, out_sb=2, out=16,
      )
        PER.update(CHAIN_N)
        sem = {n: ctx.enter_context(nc.semaphore(n)) for n in PER}
        loaded = ctx.enter_context(nc.semaphore("loaded"))
        early = ctx.enter_context(nc.semaphore("early"))
        prep = ctx.enter_context(nc.semaphore("prep"))
        n_loads = [0]

        def upto(name, i, k=None):
            return i * PER[name] + (PER[name] if k is None else k)

        passed = ctx.enter_context(nc.semaphore("passed"))

        def settle(eng):
            eng.sem_inc(passed, 1)

        class Chain:

            def __init__(self, eng, name, i):
                self.eng, self.name, self.i, self.n = eng, name, i, 0

            def __call__(self, ins, name=None):
                ins.then_inc(sem[self.name], 1)
                self.n += 1
                self.eng.wait_ge(sem[self.name], upto(self.name, self.i, self.n))
                if name:
                    self.eng.sem_inc(sem[name], 1)

            def end(self):
                assert self.n == PER[self.name], (self.name, self.n)

        V, T, SC = nc.vector, nc.tensor, nc.scalar

        SCALE = 1.0 / math.sqrt(C)

        def sp_load(sp):
            for dst, name in ((ident, "c_ident"), (gavg, "c_gavg")):
                sp.dma_start(dst[:], A[name]).then_inc(early, 16)

            def load(dst, src):
                sp.dma_start(dst, src).then_inc(loaded, 16)
                n_loads[0] += 1
            for dst, name in ((tri, "c_tri"), (later, "c_later"),
                              (t0[:, 0], "c_future")):
                load(dst[:], A[name])
            load(band[:], A["c_band"])
            load(base[:], A["c_base"])
            load(rev[:], A["c_rev"])
            load(om_w[:], A["L0_conv_om_kernel"].rearrange("a b c o -> c (a b) o"))
            load(om_b[:], A["L0_conv_om_bias"].rearrange("(a o) -> a o", a=1))
            load(conv_w[:], A["L0_conv_kernel"].rearrange("(t c) f -> c t f", c=C))
            load(conv_bias[:], A["L0_conv_bias"].rearrange("a b c f -> (a b c) f"))
            for n, w in enumerate("qkvo"):
                load(wqkvo[:, n], A["L2_attn_W" + w])
            load(bqk[:, 0:1], A["L2_attn_bq"].rearrange("(c a) -> c a", a=1))
            load(bqk[:, 1:2], A["L2_attn_bk"].rearrange("(c a) -> c a", a=1))
            load(bv_row[:], A["L2_attn_bv"].rearrange("(a c) -> a c", a=1))
            load(bo_row[:], A["L2_attn_bo"].rearrange("(a c) -> a c", a=1))
            load(router1[:], A["router1_t"])
            load(router2[:], A["router2_t"])
            load(b1[:], A["b1_t"])
            load(b2[:], A["L2_ffn_b2"])
            load(w_zdt[:], A["w_zdt_t"])
            for k in range(CONVK):
                load(w_xbc[:, k], A["w_xbc_t"])
            load(cb_row[:], A["L3_attn_conv_b"].rearrange("(a c) -> a c", a=1))
            load(dt_bias[:], A["L3_attn_dt_bias"].partition_broadcast(P))
            load(neg_a[:], A["L3_attn_A_log"].partition_broadcast(P))
            load(dskip[:], A["L3_attn_Dp"].partition_broadcast(P))
            load(gnorm[:], A["gnorm_t"])
            load(rms_w[:], A["L3_attn_norm_w"].rearrange("(c a) -> c a", a=1))
            load(w_out[:], A["w_out_t"])
            load(gath[:].rearrange("p a b q -> p (a b q)")[:, 0:CONVK * XBC],
                 A["conv_w_t"].rearrange("a b -> (a b)").partition_broadcast(P))

        def sp_zero_quads(sp):
            sp.wait_ge(prep, 1)
            flat = quads.rearrange("a b -> (a b)").rearrange("(p n) -> p n", p=P)
            n = flat.shape[1]
            step = SORT_T * TOK
            za = srt_a[:].rearrange("p a b -> p (a b)")
            for o in range(0, n, step):
                w = min(step, n - o)
                sp.dma_start(flat[:, o:o + w], za[:, 0:w]).then_inc(loaded, 16)
                n_loads[0] += 1

        def dve_prep(dve):
            V.memset(srt_a[:], 0.0)
            V.memset(ones[:], 1.0)
            V.memset(xn_pad[:], 0.0)
            V.memset(u_t[:, 0:CONVK - 1], 0.0)
            V.memset(eps_ln[:], LN_EPS)
            V.memset(one_col[:], 1.0)
            V.memset(eps_rms1[:], RMS1_EPS).then_inc(prep, 1)

        def dve_prep_late(dve):
            dve.wait_ge(early, 16 * 2)
            dve.wait_ge(loaded, 16 * n_loads[0])
            cw = gath[:].rearrange("p a b q -> p (a b q)")[:, 0:CONVK * XBC]
            V.tensor_tensor(w_xbc[:].rearrange("p k c -> p (k c)"), w_xbc[:].rearrange("p k c -> p (k c)"), cw,
                            ALU.mult).then_inc(prep, 1)
            dve.wait_ge(prep, 3)
            V.tensor_scalar(bqk[:, 0:1], bqk[:, 0:1], -SCALE, None, ALU.mult)
            V.tensor_copy(ident_h[:], ident[:])
            V.tensor_copy(future_h[:], t0[:, 0])
            V.tensor_scalar(neg_a[:], neg_a[:], -1.0, None, ALU.mult).then_inc(prep, 1)
            dve.wait_ge(prep, 4)

        def act_prep(act):
            act.wait_ge(early, 16 * 2)
            act.wait_ge(loaded, 16 * n_loads[0])
            act.wait_ge(prep, 2)
            SC.activation(neg_a[:], neg_a[:], ACT.Exp).then_inc(prep, 1)
            act.wait_ge(prep, 4)

        def others_prep(eng):
            eng.wait_ge(early, 16 * 2)
            eng.wait_ge(loaded, 16 * n_loads[0])
            eng.wait_ge(prep, 4)

        def win(t, dy=1, dx=1):
            return xn_pad[:, dx, ROWS * t + dy:ROWS * t + dy + ROWS].rearrange("p y x -> p (y x)")

        def sp_x(sp, i):
            sp.wait_ge(sem["conv"], upto("conv", i, 0))
            settle(sp)
            sp.dma_start(x_tok[:], A["x"][bass.ds(i, 1)].rearrange("a (t r) w c -> (a r w) t c", t=NT)).then_inc(sem["x_in"], 16)

        def sp_pre(sp, i):
            sp.wait_ge(sem["xn_tok"], upto("xn_tok", i, 2))
            settle(sp)
            sp.wait_ge(sem["gath0"], upto("gath0", i, 0))
            settle(sp)
            sp.wait_ge(sem["gath1"], upto("gath1", i, 0))
            settle(sp)
            q = quads.rearrange("(y x) (s c) -> y x s c", x=CELL, c=C)
            for t in range(NT):
                for dy in range(2):
                    for dx in range(2):
                        for_rows = q[ROWS * t + 1 - dy:ROWS * t + 1 - dy + ROWS, 1 - dx:1 - dx + WIDTH, 2 * dy + dx]
                        sp.dma_start(for_rows, xn_tok[:, t]).then_inc(sem["quad_out"], 16)

        def pe_gn(pe, i, n, src):
            for t in range(NT):
                ins = T.transpose(PA[t // 4][:, (t % 4) * P:(t % 4 + 1) * P], src[:, t], ident[:])
            ins.then_inc(sem["x_t"], 1)
            for k in range(2):
                yield
                pe.wait_ge(sem["gn_mom"], upto("gn_mom", i, 2 * n + k + 1))
                T.matmul(PA[2][:, 0:1], gavg[:], mv[:, (0, 4)[k]:(0, 4)[k] + 1], start=True, stop=True).then_inc(sem["gn_avg"], 1)

        def dve_gn(dve, i, n, link):
            dve.wait_ge(sem["x_t"], upto("x_t", i, n + 1))
            for h in range(2):
                ins = V.bn_stats(bst[:, h], PA[h][:])
                if h:
                    link(ins)
            settle(dve)
            link(V.bn_aggr(mv[:, 0:2], bst[:]), "gn_mom")
            yield PIECE
            dve.wait_ge(sem["gn_avg"], upto("gn_avg", i, 2 * n + 1))
            link(V.tensor_copy(mv[:, 2:3], PA[2][:, 0:1]))
            link(V.tensor_tensor(mv[:, 3:4], mv[:, 0:1], mv[:, 2:3], ALU.subtract))
            V.scalar_tensor_tensor(mv[:, 4:5], mv[:, 3:4], mv[:, 3:4], mv[:, 1:2], ALU.mult, ALU.add).then_inc(sem["gn_mom"], 1)
            yield PIECE
            dve.wait_ge(sem["gn_std"], upto("gn_std", i, n + 1))
            link(V.reciprocal(mv[:, 6:7], mv[:, 5:6]))
            V.scalar_tensor_tensor(mv[:, 7:8], mv[:, 2:3], -1.0, mv[:, 6:7], ALU.mult, ALU.mult).then_inc(sem["gn_scale"], 1)

        def act_gn(act, i, n):
            yield
            yield
            act.wait_ge(sem["gn_avg"], upto("gn_avg", i, 2 * n + 2))
            SC.activation(mv[:, 5:6], PA[2][:, 0:1], ACT.Sqrt, bias=eps_ln[:, 0:1]).then_inc(sem["gn_std"], 1)
            act.wait_ge(sem["gn_scale"], upto("gn_scale", i, n + 1))
            for h in range(2):
                if n == 0:
                    img = PA[h][:].rearrange("p (y x) -> p y x", x=WIDTH)
                    rows = xn_pad[:, :, 1 + 16 * h:17 + 16 * h]
                    moves = [(rows[:, 1], img), (rows[:, 0, :, 1:WIDTH], img[:, :, 0:WIDTH - 1]),
                             (rows[:, 2, :, 0:WIDTH - 1], img[:, :, 1:WIDTH])]
                else:
                    moves = [(yn_t[:, h * HALF:(h + 1) * HALF], PA[h][:])]
                for dst, src in moves:
                    ins = SC.activation(dst, src, ACT.Identity, bias=mv[:, 7:8], scale=mv[:, 6:7])
            ins.then_inc(sem["gn_out"], 1)

        def pe_pre(pe, i):
            pe.wait_ge(sem["x_in"], upto("x_in", i))
            pe.wait_ge(sem["corr_sb"], upto("corr_sb", i, 0))
            yield from pe_gn(pe, i, 0, x_tok)
            yield
            if isinstance(i, int) and i == 0:
                others_prep(pe)
            pe.wait_ge(sem["gn_out"], upto("gn_out", i, 1))
            om = PA[2][:, 0:NT * OM].rearrange("p (t o) -> p t o", o=OM)
            T.matmul(om, ones[0:1, :], om_b[:].unsqueeze(1).to_broadcast([1, NT, OM]), start=True, stop=False)
            for t in range(NT):
                for k in range(TAPS):
                    ins = T.matmul(om[:, t], win(t, k // 3, k % 3), om_w[:, k], start=False,
                                   stop=(t == NT - 1 and k == TAPS - 1))
            ins.then_inc(sem["om_done"], 1)
            for t in range(NT):
                ins = T.transpose(PA[t // 4][:, (t % 4) * P:(t % 4 + 1) * P], win(t), ident[:])
                if t % 4 == 3:
                    ins.then_inc(sem["xn_back"], 1)
            yield
            yield
            for g in range(NG):
                t, part = divmod(g, TAPS // TG)
                pe.wait_ge(sem["gath%d" % (g % 2)], upto("gath%d" % (g % 2), i, 16 * TG * (g // 2 + 1)))
                pe.wait_ge(sem["diag"], upto("diag", i, g + 1))
                if g < 2:
                    pe.wait_ge(sem["xn_tok"], upto("xn_tok", i, g + 1))
                else:
                    pe.wait_ge(sem["cols"], upto("cols", i, g - 1))
                for k in range(TG):
                    for s in range(4):
                        ins = T.matmul(PA[g % 2][:, k * P:(k + 1) * P], gath[:, g % 2, k, s * C:(s + 1) * C],
                                       diag[:, g % 2, 4 * k + s], start=(s == 0), stop=(s == 3))
                ins.then_inc(sem["colt"], 1)
                if part == TAPS // TG - 1:
                    pe.wait_ge(sem["cols"], upto("cols", i, g + 1))
                    if t == 0:
                        pe.wait_ge(sem["om_sb"], upto("om_sb", i))
                        pe.wait_ge(sem["sig"], upto("sig", i))
                    else:
                        pe.wait_ge(sem["x1"], upto("x1", i, t))
                    out = PA[2][:, 0:C]
                    T.matmul(out, ident[:], x_tok[:, t], start=True, stop=False)
                    T.matmul(out, ones[0:1, :], conv_bias[:], start=False, stop=False)
                    for k in range(TAPS):
                        ins = T.matmul(out, cols[:, k], conv_w[:, k], start=False, stop=(k == TAPS - 1))
                    ins.then_inc(sem["conv"], 1)
                yield
            pe.wait_ge(sem["x1"], upto("x1", i))
            yield from pe_gn(pe, i, 1, x1_tok)
            yield
            pe.wait_ge(sem["gn_out"], upto("gn_out", i, 2))

        def pe_corr(pe, i, h2):
            for t in range(SORT_T * h2, SORT_T * (h2 + 1)):
                if t:
                    pe.wait_ge(sem["corr_sb"], upto("corr_sb", i, 2 * t - 2 if t > 1 else 1))
                for h in range(2):
                    if t and h:
                        pe.wait_ge(sem["corr_sb"], upto("corr_sb", i, 2 * t - 1))
                    ins = T.matmul(PA[(2 * t + h) % 3][:], yn_t[:, t * P:(t + 1) * P], yn_t[:, h * HALF:(h + 1) * HALF],
                                   start=True, stop=True)
                ins.then_inc(sem["corr_mm"], 1)
                yield

        def act_diag(act, i, g):
            if g >= 2:
                act.wait_ge(sem["colt"], upto("colt", i, g - 1))
            w = w4[:, TG * g:TG * (g + 1)].rearrange("p k s -> p (k s)")
            for n in range(4 * TG):
                ins = SC.activation(diag[:, g % 2, n], ident[:], ACT.Copy, scale=w[:, n:n + 1])
            ins.then_inc(sem["diag"], 1)

        def act_pre(act, i):
            yield from act_gn(act, i, 0)
            if isinstance(i, int) and i == 0:
                act_prep(act)
            yield
            act.wait_ge(sem["om_done"], upto("om_done", i))
            om = PA[2][:, 0:NT * OM].rearrange("p (t o) -> p t o", o=OM)
            SC.activation(oms[:], om, ACT.Identity).then_inc(sem["om_sb"], 1)
            SC.activation(mask[:], om[:, :, 2 * TAPS:OM], ACT.Sigmoid).then_inc(sem["sig"], 1)
            for h in range(2):
                act.wait_ge(sem["xn_back"], upto("xn_back", i, h + 1))
                if h == 0:
                    act.wait_ge(sem["quad_out"], upto("quad_out", i, 0))
                SC.activation(xn_tok[:, 4 * h:4 * h + 4].rearrange("p t c -> p (t c)"), PA[h][:], ACT.Identity).then_inc(sem["xn_tok"], 1)
            yield
            yield
            for g in range(NG):
                if g == 0:
                    act.wait_ge(sem["w4"], upto("w4", i))
                    act_diag(act, i, 0)
                    act_diag(act, i, 1)
                t, part = divmod(g, TAPS // TG)
                act.wait_ge(sem["colt"], upto("colt", i, g + 1))
                if part == 0 and t:
                    act.wait_ge(sem["conv"], upto("conv", i, t))
                SC.activation(cols[:, TG * part:TG * (part + 1)].rearrange("p k c -> p (k c)"),
                                   PA[g % 2][:, 0:TG * P], ACT.Identity).then_inc(sem["cols"], 1)
                if part == TAPS // TG - 1:
                    act.wait_ge(sem["conv"], upto("conv", i, t + 1))
                    if t == 0:
                        act.wait_ge(sem["quad_out"], upto("quad_out", i))
                    SC.activation(x1_tok[:, t], PA[2][:, 0:C], ACT.Identity).then_inc(sem["x1"], 1)
                if g + 2 < NG:
                    act_diag(act, i, g + 2)
                yield
            yield from act_gn(act, i, 1)
            yield

        def act_corr(act, i, h2):
            for t in range(SORT_T * h2, SORT_T * (h2 + 1)):
                act.wait_ge(sem["corr_mm"], upto("corr_mm", i, t + 1))
                if t % SORT_T == 0:
                    act.wait_ge(sem["corr_used"], upto("corr_used", i, h2))
                for h in range(2):
                    SC.activation(corr[:, t % SORT_T, h * HALF:(h + 1) * HALF], PA[(2 * t + h) % 3][:],
                                       ACT.Identity, scale=1.0 / C).then_inc(sem["corr_sb"], 1)
                yield

        def dve_pre(dve, i):
            link = Chain(dve, "dve_pre", i)
            yield from dve_gn(dve, i, 0, link)
            if isinstance(i, int) and i == 0:
                dve_prep_late(dve)
            yield PIECE
            yield PIECE
            dve.wait_ge(sem["om_sb"], upto("om_sb", i))
            off = oms[:, :, 0:2 * TAPS].rearrange("p t (k d) -> p t k d", d=2)
            for d in range(2):
                ins = V.tensor_tensor(pos[:, d].rearrange("p (t k) -> p t k", k=TAPS),
                                      base[:, d].rearrange("p (t k) -> p t k", k=TAPS), off[:, :, :, d], ALU.add)
            link(ins)
            link(V.tensor_scalar(pos[:], pos[:], 0.0, float(HEIGHT + 1), ALU.max, ALU.min))
            link(V.tensor_copy(posi[:], pos[:]))
            link(V.tensor_copy(cell[:], posi[:]))
            link(V.tensor_tensor(gt[:], cell[:], pos[:], ALU.is_gt))
            link(V.tensor_tensor(cell[:], cell[:], gt[:], ALU.subtract))
            dve.wait_ge(sem["gath0"], upto("gath0", i, 0))
            dve.wait_ge(sem["gath1"], upto("gath1", i, 0))
            V.scalar_tensor_tensor(idx[:], cell[:, 0], float(CELL), cell[:, 1], ALU.mult, ALU.add).then_inc(sem["idx"], 1)
            link(V.tensor_tensor(frac[:, 1], pos[:], cell[:], ALU.subtract))
            link(V.tensor_scalar(frac[:, 0], frac[:, 1], -1.0, 1.0, ALU.mult, ALU.add))
            dve.wait_ge(sem["sig"], upto("sig", i))
            for r in range(2):
                ins = V.scalar_tensor_tensor(wym[:, r], mask[:].rearrange("p t k -> p (t k)"), 2.0, frac[:, r, 0],
                                             ALU.mult, ALU.mult)
            link(ins)
            dve.wait_ge(sem["diag"], upto("diag", i, 0))
            for r in range(2):
                for c in range(2):
                    ins = V.tensor_tensor(w4[:, :, 2 * r + c], wym[:, r], frac[:, c, 1], ALU.mult)
            ins.then_inc(sem["w4"], 1)
            yield PIECE
            for g in range(NG):
                yield PIECE
            yield from dve_gn(dve, i, 1, link)
            link.end()
            yield PIECE
            for t in range(SORT_T):
                yield PIECE

        def pool_pre(pool, i):
            def gather(g):
                if g >= 2:
                    pool.wait_ge(sem["colt"], upto("colt", i, g - 1))
                    settle(pool)
                for k in range(TG):
                    pool.indirect_dma_start(gath[:, g % 2, k], None, quads,
                                            bass.IndirectOffsetOnAxis(idx[:, TG * g + k:TG * g + k + 1], 0)
                                                 ).then_inc(sem["gath%d" % (g % 2)], 16)

            for _ in range(3):
                yield
            pool.wait_ge(sem["idx"], upto("idx", i))
            settle(pool)
            pool.wait_ge(sem["quad_out"], upto("quad_out", i))
            settle(pool)
            gather(0)
            gather(1)
            for g in range(NG):
                if g + 2 < NG:
                    gather(g + 2)
                yield
            for _ in range(1 + SORT_T):
                yield

        def dve_sort(dve, i, h, link):
            dve.wait_ge(sem["corr_sb"], upto("corr_sb", i, 2 * SORT_T * (h + 1)))
            bufs = (srt_a, srt_b)

            def compare(size, src, dst, name=None):
                lo, hi = src[:, :, 0:size // 2], src[:, :, size // 2:size]
                if size == TOK:
                    hi = hi[:, :, ::-1]
                V.tensor_tensor(dst[:, :, 0:size // 2], lo, hi, ALU.max)
                yield
                link(V.tensor_tensor(dst[:, :, size // 2:size], lo, hi, ALU.min), name)
                yield

            def runs(buf, m):
                return buf[:].rearrange("p g (b m) -> p (g b) m", m=m)

            yield from compare(2, runs(corr, 2), runs(srt_a, 2), "corr_used")
            now = 0
            m = 4
            while m < TOK:
                yield from compare(m, runs(bufs[now], m), runs(bufs[1 - now], m))
                now = 1 - now
                here, there = runs(bufs[now], m), runs(bufs[1 - now], m)
                k = m // 4
                if m > 4:
                    lo, hi = here[:, :, k:2 * k], here[:, :, 2 * k:3 * k]
                    V.tensor_tensor(there[:, :, k:2 * k], lo, hi, ALU.max)
                    link(V.tensor_tensor(there[:, :, 2 * k:3 * k], lo, hi, ALU.min))
                    yield
                    k //= 2

                    def eighth(buf, e):
                        return buf[:, :, e * k:(e + 1) * k]

                    for e, a, b in ((1, here, there), (3, there, there), (5, there, here)):
                        lo, hi = eighth(a, e), eighth(b, e + 1)
                        ops = [(e, ALU.max), (e + 1, ALU.min)]
                        for out, side in (reversed(ops) if e == 1 else ops):
                            ins = V.tensor_tensor(eighth(here, out), lo, hi, side)
                        if e == 3:
                            yield
                    link(ins)
                    yield
                    k //= 2
                while k >= 1:
                    x, y = (b[:, :, k:m - k].rearrange("p r (c s k) -> p r c s k", s=2, k=k) for b in (here, there))
                    V.tensor_tensor(y[:, :, :, 0], x[:, :, :, 0], x[:, :, :, 1], ALU.max)
                    yield
                    V.tensor_tensor(y[:, :, :, 1], x[:, :, :, 0], x[:, :, :, 1], ALU.min)
                    x, y = (b.rearrange("p r (c k) -> p r c k", k=k)[:, :, ::m // k - 1] for b in (here, there))
                    link(V.tensor_copy(y, x))
                    yield
                    now = 1 - now
                    here, there = there, here
                    k //= 2
                m *= 2
            k = TOK
            while k >= 16:
                yield from compare(k, runs(bufs[now], k), runs(bufs[1 - now], k))
                now = 1 - now
                k //= 2
            src, stage = bufs[now], 1 - now
            for k in (4, 2, 1):
                dst = bufs[stage % 2]
                last = k == 1
                for c, cnt, r in rank_pieces():
                    base_r = r // (2 * k) * (2 * k)
                    side = ALU.max if (r % (2 * k)) < k else ALU.min
                    lo = bass_slice(src, base_r, cnt, k)
                    hi = bass_slice(src, base_r + k, cnt, k)
                    if last:
                        out = dst[:, :, c:c + cnt].unsqueeze(3)
                    else:
                        out = bass_slice(dst, r // k * k, cnt, k)
                    ins = V.tensor_tensor(out, lo, hi, side)
                link(ins)
                yield
                src = dst
                stage += 1
            if h == 0:
                dve.wait_ge(sem["x2_copy"], upto("x2_copy", i))
            x2 = x2_tok[:, SORT_T * h:SORT_T * (h + 1)]
            link(V.tensor_tensor(x2, x2, src[:, :, 0:C], ALU.add), "ranked")

        def bass_slice(buf, start, cnt, k):
            cells = buf[:].rearrange("p g (b e) -> p g b e", e=8)
            return cells[:, :, start // 8:start // 8 + cnt, start % 8:start % 8 + k]

        def ln_stats(dve, i, n, src, link):
            for t in range(NT):
                ins = V.bn_stats(lnst[:, t], src[:, t])
            link(ins)
            settle(dve)
            for t in range(NT):
                ins = V.bn_aggr(lnmv[:, t], lnst[:, t:t + 1])
            link(ins)
            link(V.tensor_scalar(lnsd[:, 0], lnmv[:, :, 1], LN_EPS, None, ALU.add), "ln_v")
            yield PIECE
            dve.wait_ge(sem["ln_std"], upto("ln_std", i, n + 1))
            link(V.reciprocal(lnsd[:, 1], lnsd[:, 0]))
            for t in range(NT):
                ins = V.tensor_scalar(u[:, t], src[:, t], lnmv[:, t, 0:1], lnsd[:, 1, t:t + 1], ALU.subtract, ALU.mult)
            ins.then_inc(sem["ln_u"], 1)

        def act_ln(act, i, n, transposed=True):
            act.wait_ge(sem["ln_v"], upto("ln_v", i, n + 1))
            SC.activation(lnsd[:, 0], lnsd[:, 0], ACT.Sqrt).then_inc(sem["ln_std"], 1)
            yield
            if transposed:
                for h in range(2):
                    act.wait_ge(sem["ln_ut"], upto("ln_ut", i, 2 * (n - n // 3) + h + 1))
                    SC.activation(u_t[:, 3 + h * HALF:3 + (h + 1) * HALF], PB[h][:], ACT.Identity).then_inc(sem["ln_utsb"], 1)

        def pe_ln(pe, i, n):
            pe.wait_ge(sem["ln_u"], upto("ln_u", i, n + 1))
            for t in range(NT):
                ins = T.transpose(PB[t // 4][:, (t % 4) * P:(t % 4 + 1) * P], u[:, t], ident[:])
                if t % 4 == 3:
                    ins.then_inc(sem["ln_ut"], 1)

        def utile(t):
            return u_t[:, 3 + t * P:3 + (t + 1) * P]

        def uhalf(h):
            return u_t[:, 3 + h * HALF:3 + (h + 1) * HALF]

        def flat4(buf, h):
            return buf[:, 4 * h:4 * h + 4].rearrange("p t c -> p (t c)")

        def row4(row):
            return row.unsqueeze(1).to_broadcast([1, 4, C])


        def pe_att(pe, i):
            yield
            pe_ln(pe, i, 0)
            yield
            pe.wait_ge(sem["ln_utsb"], upto("ln_utsb", i, 2))
            for h in range(2):
                ins = T.matmul(PB[h][:], wqkvo[:, 0], uhalf(h), start=True, stop=True)
            ins.then_inc(sem["qkv"], 1)
            for h in range(2):
                ins = T.matmul(PB[2 + h][:], wqkvo[:, 1], uhalf(h), start=True, stop=True)
            ins.then_inc(sem["qkv"], 1)
            yield
            pe.wait_ge(sem["qkv_sb"], upto("qkv_sb", i, 1))
            for h in range(2):
                T.matmul(PB[h][:], ones[0:1, :], row4(bv_row[:]), start=True, stop=False)
                for t in range(4):
                    ins = T.matmul(PB[h][:, t * P:(t + 1) * P], utile(4 * h + t), wqkvo[:, 2], start=False,
                                   stop=(t == 3))
            ins.then_inc(sem["qkv"], 1)
            pe.wait_ge(sem["qkv_sb"], upto("qkv_sb", i, 2))
            T.matmul(PB[2][:, 0:C], ones[0:1, :], bv_row[:], start=True, stop=True).then_inc(sem["qkv"], 1)
            yield
            pe.wait_ge(sem["qkv_sb"], upto("qkv_sb", i, 4))

            def scores(t):
                if t >= 2:
                    pe.wait_ge(sem["masked"], upto("masked", i, t - 1))
                T.matmul(PB[t % 2][:, 0:KEYS], q_t[:, t * P:(t + 1) * P], k_t[:, t * P:t * P + KEYS],
                              start=True, stop=True).then_inc(sem["score"], 1)
            scores(0)
            yield
            for t in range(1, NT + 3):
                if t < NT:
                    scores(t)
                if 3 <= t:
                    n = t - 3
                    pe.wait_ge(sem["prob_sb"], upto("prob_sb", i, n + 1))
                    if n:
                        pe.wait_ge(sem["ctx_sb"], upto("ctx_sb", i, n))
                    for s in range(2):
                        ins = T.matmul(PB[3][:, 0:P], v_tok[:, n + s], prob_t[:, s * P:(s + 1) * P],
                                       start=(s == 0), stop=(s == 1))
                    ins.then_inc(sem["ctx_ps"], 1)
                if 2 <= t < NT + 2:
                    n = t - 2
                    pe.wait_ge(sem["probd"], upto("probd", i, n + 1))
                    if n:
                        pe.wait_ge(sem["prob_sb"], upto("prob_sb", i, n))
                    for s in range(2):
                        ins = T.transpose(PB[2][:, s * P:(s + 1) * P], prob[:, s * P:(s + 1) * P], ident[:])
                    ins.then_inc(sem["prob_ps"], 1)
                yield
            pe.wait_ge(sem["ctx_sb"], upto("ctx_sb", i))
            for h in range(2):
                T.matmul(PB[h][:], ident[:], flat4(t0, h), start=True, stop=False)
                T.matmul(PB[h][:], ident[:], flat4(u, h), start=False, stop=False)
                T.matmul(PB[h][:], ones[0:1, :], row4(bo_row[:]), start=False, stop=False)
                for t in range(4):
                    n = 4 * h + t
                    ins = T.matmul(PB[h][:, t * P:(t + 1) * P], ctx_t[:, n * P:(n + 1) * P], wqkvo[:, 3],
                                   start=False, stop=(t == 3))
                ins.then_inc(sem["att_out"], 1)
            yield

        def act_att(act, i):
            yield from act_ln(act, i, 0)
            yield
            act.wait_ge(sem["qkv"], upto("qkv", i, 1))
            for h in range(2):
                ins = SC.activation(q_t[:, h * HALF:(h + 1) * HALF], PB[h][:], ACT.Identity, bias=bqk[:, 0:1],
                                    scale=-SCALE)
            ins.then_inc(sem["qkv_sb"], 1)
            act.wait_ge(sem["qkv"], upto("qkv", i, 2))
            for h in range(2):
                SC.activation(k_t[:, BACK + h * HALF:BACK + (h + 1) * HALF], PB[2 + h][:], ACT.Identity,
                              bias=bqk[:, 1:2])
            SC.activation(k_t[:, 0:BACK], ident[:, 0:BACK], ACT.Identity, bias=bqk[:, 1:2], scale=0.0).then_inc(sem["qkv_sb"], 1)
            yield
            act.wait_ge(sem["qkv"], upto("qkv", i, 3))
            for h in range(2):
                ins = SC.activation(v_tok[:, 1 + 4 * h:5 + 4 * h].rearrange("p t c -> p (t c)"), PB[h][:], ACT.Identity)
            ins.then_inc(sem["qkv_sb"], 1)
            act.wait_ge(sem["qkv"], upto("qkv", i, 4))
            SC.activation(v_tok[:, 0], PB[2][:, 0:C], ACT.Identity).then_inc(sem["qkv_sb"], 1)
            SC.activation(prob[:, 0:P - BACK], ident[:, 0:P - BACK], ACT.Identity, scale=0.0).then_inc(sem["qkv_sb"], 1)
            yield
            yield
            for t in range(1, NT + 3):
                if t <= NT:
                    n = t - 1
                    act.wait_ge(sem["masked"], upto("masked", i, n + 1))
                    if n >= 2:
                        act.wait_ge(sem["probd"], upto("probd", i, n - 1))
                    for w in range(3):
                        ins = SC.activation(ex[n % 2][:, w], sm[n % 2][:, w], ACT.Exp, bias=nmax[n % 2][:, w:w + 1],
                                            scale=-1.0, accum_out=asum[n % 2][:, w:w + 1])
                    ins.then_inc(sem["expd"], 1)
                if t >= 3:
                    n = t - 3
                    act.wait_ge(sem["ctx_ps"], upto("ctx_ps", i, n + 1))
                    SC.activation(ctx_t[:, n * P:(n + 1) * P], PB[3][:, 0:P], ACT.Identity,
                                       scale=1.0 / len(WINDOWS)).then_inc(sem["ctx_sb"], 1)
                if 2 <= t < NT + 2:
                    n = t - 2
                    act.wait_ge(sem["prob_ps"], upto("prob_ps", i, n + 1))
                    if n:
                        act.wait_ge(sem["ctx_ps"], upto("ctx_ps", i, n))
                    SC.activation(prob_t[:], PB[2][:, 0:2 * P], ACT.Identity).then_inc(sem["prob_sb"], 1)
                yield
            for h in range(2):
                act.wait_ge(sem["att_out"], upto("att_out", i, h + 1))
                SC.activation(flat4(t1, h), PB[h][:], ACT.Identity).then_inc(sem["t1"], 1)
            yield

        def dve_att(dve, i, link):
            yield from ln_stats(dve, i, 0, t0, link)
            for _ in range(3):
                yield PIECE

            def masked(t):
                dve.wait_ge(sem["score"], upto("score", i, t + 1))
                if t >= 2:
                    dve.wait_ge(sem["expd"], upto("expd", i, t - 1))
                link(V.tensor_tensor(sm[t % 2][:], PB[t % 2][:, 0:KEYS].unsqueeze(1).to_broadcast([P, 3, KEYS]),
                                     band[:], ALU.add))
                V.tensor_reduce(nmax[t % 2][:], sm[t % 2][:], AX.X, ALU.min).then_inc(sem["masked"], 1)

            masked(0)
            yield PIECE
            for t in range(1, NT + 3):
                if t < NT:
                    masked(t)
                if t <= NT:
                    n = t - 1
                    yield GAP["att"]
                    dve.wait_ge(sem["expd"], upto("expd", i, n + 1))
                    if n:
                        dve.wait_ge(sem["probd"], upto("probd", i, n))
                    link(V.reciprocal(arec[:], asum[n % 2][:]))
                    if n:
                        dve.wait_ge(sem["prob_ps"], upto("prob_ps", i, n))
                    else:
                        dve.wait_ge(sem["qkv_sb"], upto("qkv_sb", i, 5))
                    p, e = prob[:, P - BACK:2 * P], ex[n % 2]
                    link(V.tensor_scalar(p, e[:, 0], arec[:, 0:1], None, ALU.mult))
                    link(V.scalar_tensor_tensor(p, e[:, 1], arec[:, 1:2], p, ALU.mult, ALU.add))
                    V.scalar_tensor_tensor(p, e[:, 2], arec[:, 2:3], p, ALU.mult, ALU.add).then_inc(sem["probd"], 1)
                yield PIECE
            yield PIECE

        def pe_logits(pe, i, n, router):
            pe.wait_ge(sem["ln_utsb"], upto("ln_utsb", i, (4, 6)[n]))
            for t in range(NT):
                ins = T.matmul(PB[2][:, t * E8:(t + 1) * E8], utile(t), router[:], start=True, stop=True)
            ins.then_inc(sem["logit"], 1)

        def act_route(act, i, n):
            act.wait_ge(sem["g_e"], upto("g_e", i, n + 1))
            SC.activation(gp[:], gl[:], ACT.Exp).then_inc(sem["g_exp"], 1)

        def dve_route(dve, i, n, link):
            def ex8(row):
                return gsm[:, row].unsqueeze(2).to_broadcast([P, NT, E8])
            yield GAP["logit"]
            dve.wait_ge(sem["logit"], upto("logit", i, n + 1))
            link(V.tensor_copy(gl[:], PB[2][:, 0:NT * E8].rearrange("p (t e) -> p t e", e=E8)))
            link(V.tensor_reduce(gsm[:, 0], gl[:], AX.X, ALU.max))
            V.tensor_tensor(gl[:], gl[:], ex8(0), ALU.subtract).then_inc(sem["g_e"], 1)
            yield GAP["gate"]
            dve.wait_ge(sem["g_exp"], upto("g_exp", i, n + 1))
            link(V.tensor_reduce(gsm[:, 1], gp[:], AX.X, ALU.add))
            link(V.reciprocal(gsm[:, 2], gsm[:, 1]))
            link(V.tensor_tensor(gp[:], gp[:], ex8(2), ALU.mult))
            p, revb = gp, rev[:].unsqueeze(1).to_broadcast([P, NT, E8])
            for k, oh in enumerate((oh1, oh2)):
                link(V.tensor_reduce(gsm[:, 3 + k], p[:], AX.X, ALU.max))
                link(V.tensor_tensor(gv[:], p[:], ex8(3 + k), ALU.is_equal))
                link(V.tensor_tensor(gv[:], gv[:], revb, ALU.mult))
                link(V.tensor_reduce(gsm[:, 5], gv[:], AX.X, ALU.max))
                link(V.tensor_tensor(oh[:], gv[:], ex8(5), ALU.is_equal))
                if k == 0:
                    link(V.scalar_tensor_tensor(gq[:], oh1[:], -2.0, gp[:], ALU.mult, ALU.add))
                    p = gq
            link(V.tensor_tensor(gsm[:, 6], gsm[:, 3], gsm[:, 4], ALU.add))
            if n == 0:
                link(V.tensor_scalar(gsm[:, 6], gsm[:, 6], 1e-12, None, ALU.max))
            else:
                link(V.tensor_scalar(gsm[:, 6], gsm[:, 6], 1e-9, None, ALU.add))
            link(V.reciprocal(gsm[:, 7], gsm[:, 6]))
            link(V.tensor_tensor(oh1[:], oh1[:], ex8(3), ALU.mult))
            link(V.tensor_tensor(oh2[:], oh2[:], ex8(4), ALU.mult))
            link(V.tensor_tensor(oh1[:], oh1[:], oh2[:], ALU.add))
            V.tensor_tensor(gates[:], oh1[:], ex8(7), ALU.mult).then_inc(sem["gated"], 1)

        def pe_gate_rows(pe, out, h, e):
            for t in range(4):
                ins = T.matmul(out[:, t * P:(t + 1) * P], gates[:, 4 * h + t, e:e + 1].to_broadcast([P, P]), ident[:],
                               start=True, stop=True)
            return ins

        def sp_e1(sp, i):
            for e in range(E8):
                if e >= 3:
                    sp.wait_ge(sem["y1_ps"], upto("y1_ps", i, 2 * (e - 2)))
                    settle(sp)
                sp.dma_start(e1w[:, e % 3, 0], A["L2_ffn_w1"][e]).then_inc(sem["e1_in%d" % (e % 3)], 16)
                sp.dma_start(e1w[:, e % 3, 1], A["L2_ffn_w2"][e]).then_inc(sem["e1_in%d" % (e % 3)], 16)

        def pe_moe1(pe, i):
            pe.wait_ge(sem["t1"], upto("t1", i))
            yield
            pe_ln(pe, i, 1)
            yield
            pe_logits(pe, i, 0, router1)
            yield
            pe.wait_ge(sem["gated"], upto("gated", i, 1))
            for h in range(2):
                for t in range(4):
                    ins = T.transpose(PB[h][0:E8, t * P:(t + 1) * P], gates[:, 4 * h + t], ident[:])
                ins.then_inc(sem["gt_ps"], 1)
            pe.wait_ge(sem["gt_sb"], upto("gt_sb", i))
            for h in range(2):
                T.matmul(PB[2 + h][:], ident[:], flat4(t1, h), start=True, stop=False)
                T.matmul(PB[2 + h][:], ident[:], flat4(u, h), start=False, stop=False)
                for t in range(4):
                    n = 4 * h + t
                    T.matmul(PB[2 + h][:, t * P:(t + 1) * P], gates_t[0:E8, n * P:(n + 1) * P], b2[:],
                             start=False, stop=False)
            yield
            for n in range(2 * E8 + LAG1):
                if n < 2 * E8:
                    e, h = divmod(n, 2)
                    pe.wait_ge(sem["e1_in%d" % (e % 3)], upto("e1_in%d" % (e % 3), i, 32 * (e // 3 + 1)))
                    if n:
                        pe.wait_ge(sem["gelu"], upto("gelu", i, n))
                    T.matmul(PB[0][:], e1w[:, e % 3, 0], uhalf(h), start=True, stop=True).then_inc(sem["h_ps"], 1)
                    if n >= 2:
                        pe.wait_ge(sem["gh"], upto("gh", i, n - 1))
                    pe_gate_rows(pe, GB[n % 2], h, e).then_inc(sem["gb_ps"], 1)
                if n >= LAG1:
                    e, h = divmod(n - LAG1, 2)
                    pe.wait_ge(sem["gh"], upto("gh", i, n - LAG1 + 1))
                    for t in range(4):
                        ins = T.matmul(PB[2 + h][:, t * P:(t + 1) * P], gated_h[:, (n - LAG1) % SLOTS, t * P:(t + 1) * P],
                                       e1w[:, e % 3, 1], start=False, stop=(e == E8 - 1 and t == 3))
                    ins.then_inc(sem["y1_ps"], 1)
                yield

        def act_moe1(act, i):
            yield from act_ln(act, i, 1)
            yield
            act_route(act, i, 0)
            yield
            for h in range(2):
                act.wait_ge(sem["gt_ps"], upto("gt_ps", i, h + 1))
                SC.activation(gates_t[0:E8, h * HALF:(h + 1) * HALF], PB[h][0:E8, :], ACT.Identity).then_inc(sem["gt_sb"], 1)
            yield
            for n in range(2 * E8 + LAG1):
                if n < 2 * E8:
                    e, h = divmod(n, 2)
                    act.wait_ge(sem["h_ps"], upto("h_ps", i, n + 1))
                    if n >= SLOTS:
                        act.wait_ge(sem["y1_ps"], upto("y1_ps", i, n - SLOTS + 1))
                    SC.activation(act_h[:, n % SLOTS], PB[0][:], ACT.Gelu, bias=b1[:, e:e + 1]).then_inc(sem["gelu"], 1)
                yield
            for h in range(2):
                act.wait_ge(sem["y1_ps"], upto("y1_ps", i, 15 + h))
                SC.activation(flat4(t0, h), PB[2 + h][:], ACT.Identity).then_inc(sem["t2"], 1)

        def dve_moe1(dve, i, link):
            dve.wait_ge(sem["t1"], upto("t1", i))
            yield from ln_stats(dve, i, 1, t1, link)
            yield PIECE
            yield from dve_route(dve, i, 0, link)
            yield PIECE
            yield PIECE
            for n in range(2 * E8 + LAG1):
                if 1 <= n <= 2 * E8:
                    m = n - 1
                    dve.wait_ge(sem["gelu"], upto("gelu", i, m + 1))
                    dve.wait_ge(sem["gb_ps"], upto("gb_ps", i, m + 1))
                    V.tensor_tensor(gated_h[:, m % SLOTS], act_h[:, m % SLOTS], GB[m % 2][:], ALU.mult).then_inc(sem["gh"], 1)
                yield PIECE

        def heads(ap):
            return ap.rearrange("p (h d) -> p h d", d=HDIM)

        def hb(ap, n=HDIM):
            return ap.unsqueeze(2).to_broadcast([ap.shape[0], HEADS, n])

        def steps_of(c):
            return t1[:].rearrange("p t c -> p (t c)") if c % 2 == 0 else u_t[:, 3:3 + TOK]

        def pe_ssm(pe, i):
            yield
            yield
            pe.wait_ge(sem["xn3"], upto("xn3", i))
            for t in range(NT):
                ins = T.transpose(PB[t // 4][:, (t % 4) * P:(t % 4 + 1) * P], t1[:, t], ident[:])
                if t % 4 == 3:
                    ins.then_inc(sem["xn3_ps"], 1)
            yield
            pe.wait_ge(sem["xn3_t"], upto("xn3_t", i))
            for t in range(NT):
                if t >= 2:
                    pe.wait_ge(sem["z_sb"], upto("z_sb", i, t - 1))
                    pe.wait_ge(sem["xbc_sb"], upto("xbc_sb", i, t - 1))
                T.matmul(PB[t % 2][:, 0:ZDT], utile(t), w_zdt[:], start=True, stop=True).then_inc(sem["z_ps"], 1)
                out = PB[2 + t % 2][:, 0:XBC]
                T.matmul(out, ones[0:1, :], cb_row[:], start=True, stop=False)
                for k in range(CONVK):
                    ins = T.matmul(out, u_t[:, t * P + k:t * P + k + P], w_xbc[:, k], start=False, stop=(k == CONVK - 1))
                ins.then_inc(sem["x_ps"], 1)
                yield
            pe.wait_ge(sem["z_sb"], upto("z_sb", i))
            pe.wait_ge(sem["xbc_sb"], upto("xbc_sb", i))
            for n in range(4):
                m, h = divmod(n, 2)
                for t in range(4):
                    ins = T.transpose(PB[n][0:STATE, t * P:(t + 1) * P],
                                      xbc[:, 4 * h + t, INNER + m * STATE:INNER + (m + 1) * STATE], ident[:])
                ins.then_inc(sem["bc_ps"], 1)
            yield
            yield
            pe.wait_ge(sem["la"], upto("la", i))
            pe.wait_ge(sem["bc_sb"], upto("bc_sb", i))
            laf = la[:].rearrange("p t h -> p (t h)")
            n64 = NT * HEADS
            T.matmul(PB[0][:, 0:n64], tri[:], laf, start=True, stop=True)
            T.matmul(PB[0][:, n64:2 * n64], later[:], laf, start=True, stop=True)
            T.matmul(PB[0][:, 2 * n64:3 * n64], ones[:], laf, start=True, stop=True).then_inc(sem["cum"], 1)
            yield
            pe.wait_ge(sem["ecum"], upto("ecum", i))

            def seg(c):
                pe.wait_ge(sem["steps"], upto("steps", i, c + 1))
                if c:
                    pe.wait_ge(sem["decay"], upto("decay", i, c))
                for h in range(2):
                    T.matmul(PB[h][:], ident_h[:], future_h[:].unsqueeze(1).to_broadcast([P, 4, P]), start=True,
                             stop=False)
                    ins = T.matmul(PB[h][:], later[:], steps_of(c)[:, h * HALF:(h + 1) * HALF], start=False, stop=True)
                ins.then_inc(sem["seg"], 1)

            seg(0)
            yield
            for c in range(NT):
                if c:
                    pe.wait_ge(sem["state"], upto("state", i, c))
                T.matmul(PB[2][:, 0:P], b_t[0:STATE, c * P:(c + 1) * P], c_t[0:STATE, c * P:(c + 1) * P],
                              start=True, stop=True).then_inc(sem["cbt"], 1)
                if c + 1 < NT:
                    seg(c + 1)
                yield
                pe.wait_ge(sem["mix"], upto("mix", i, c + 1))
                pe.wait_ge(sem["xdr"], upto("xdr", i, c + 1))
                T.matmul(PB[2][0:STATE, 0:INNER], xbc[:, c, INNER:INNER + STATE], xdr[:], start=True, stop=True).then_inc(sem["ds_ps"], 1)
                if c:
                    pe.wait_ge(sem["y_sb"], upto("y_sb", i, c))
                for h in range(HEADS):
                    T.matmul(PB[3][:, h * HDIM:(h + 1) * HDIM], mix[:, h], xdt[:, h * HDIM:(h + 1) * HDIM],
                             start=True, stop=True)
                T.matmul(PB[3][:, INNER:2 * INNER], c_t[0:STATE, c * P:(c + 1) * P], state[:],
                              start=True, stop=True).then_inc(sem["y_ps"], 1)
                yield
            pe.wait_ge(sem["yn"], upto("yn", i))
            pe.wait_ge(sem["state"], upto("state", i))
            pe.wait_ge(sem["y_sb"], upto("y_sb", i))
            for n in range(4):
                a, h = divmod(n, 2)
                for t in range(4):
                    ins = T.transpose(PB[n][:, t * P:(t + 1) * P], ys[:, 4 * h + t, a * P:(a + 1) * P], ident[:])
                ins.then_inc(sem["yt_ps"], 1)
            yield
            pe.wait_ge(sem["yt_sb"], upto("yt_sb", i))
            for h in range(2):
                for t in range(4):
                    n = 4 * h + t
                    for a in range(2):
                        ins = T.matmul(PB[h][:, t * P:(t + 1) * P], y_t[:, a, n * P:(n + 1) * P], w_out[:, a],
                                       start=(a == 0), stop=(a == 1))
                ins.then_inc(sem["o_ps"], 1)
            yield

        def act_ssm(act, i):
            yield from act_ln(act, i, 2, transposed=False)
            act.wait_ge(sem["ln_u"], upto("ln_u", i, 3))
            for t in range(NT):
                ins = SC.activation(t1[:, t], u[:, t], ACT.Square, accum_out=rms[:, 0, t:t + 1])
            ins.then_inc(sem["rms_sq"], 1)
            act.wait_ge(sem["rms_sq"], upto("rms_sq", i, 1))
            SC.activation(rms[:, 1], rms[:, 0], ACT.Sqrt, scale=1.0 / C, bias=eps_rms1[:, 0:1]).then_inc(sem["rms_std"], 1)
            yield
            act.wait_ge(sem["rms_r"], upto("rms_r", i, 1))
            for t in range(NT):
                ins = SC.activation(t1[:, t], u[:, t], ACT.Copy, scale=rms[:, 2, t:t + 1])
            ins.then_inc(sem["xn3"], 1)
            for h in range(2):
                act.wait_ge(sem["xn3_ps"], upto("xn3_ps", i, h + 1))
                SC.activation(uhalf(h), PB[h][:], ACT.Identity, scale=rms_w[:, 0:1]).then_inc(sem["xn3_t"], 1)
            yield
            for t in range(NT):
                act.wait_ge(sem["z_ps"], upto("z_ps", i, t + 1))
                SC.activation(zs[:, t], PB[t % 2][:, 0:INNER], ACT.Silu)
                SC.activation(dtr[:, t], PB[t % 2][:, INNER:ZDT], ACT.Identity).then_inc(sem["z_sb"], 1)
                act.wait_ge(sem["x_ps"], upto("x_ps", i, t + 1))
                SC.activation(xbc[:, t], PB[2 + t % 2][:, 0:XBC], ACT.Silu).then_inc(sem["xbc_sb"], 1)
                yield
            for n in range(4):
                m, h = divmod(n, 2)
                act.wait_ge(sem["bc_ps"], upto("bc_ps", i, n + 1))
                SC.activation((b_t, c_t)[m][0:STATE, h * HALF:(h + 1) * HALF], PB[n][0:STATE, :],
                                   ACT.Identity).then_inc(sem["bc_sb"], 1)
            yield
            act.wait_ge(sem["dt_abs"], upto("dt_abs", i))
            SC.activation(dtx[:, 2], dtx[:, 1], ACT.Exp, scale=-1.0).then_inc(sem["dt_exp"], 1)
            yield
            act.wait_ge(sem["dt_w"], upto("dt_w", i))
            SC.activation(dtx[:, 4], dtx[:, 3], ACT.Ln).then_inc(sem["dt_ln"], 1)
            act.wait_ge(sem["cum"], upto("cum", i))
            SC.activation(ecum[:].rearrange("p a b -> p (a b)"), PB[0][:, 0:3 * NT * HEADS], ACT.Exp).then_inc(sem["ecum"], 1)
            yield

            def steps(c):
                if c >= 2:
                    act.wait_ge(sem["seg"], upto("seg", i, c - 1))
                for h in range(HEADS):
                    ins = SC.activation(steps_of(c)[:, h * P:(h + 1) * P], tri[:], ACT.Copy, scale=la[:, c, h:h + 1])
                ins.then_inc(sem["steps"], 1)

            act.wait_ge(sem["la"], upto("la", i))
            steps(0)
            yield
            for c in range(NT):
                if c + 1 < NT:
                    steps(c + 1)
                act.wait_ge(sem["seg"], upto("seg", i, c + 1))
                if c:
                    act.wait_ge(sem["mix"], upto("mix", i, c))
                for h in range(2):
                    ins = SC.activation(decay[:, 4 * h:4 * h + 4].rearrange("p h i -> p (h i)"), PB[h][:], ACT.Exp)
                ins.then_inc(sem["decay"], 1)
                yield
                yield
            act.wait_ge(sem["yn"], upto("yn", i))
            for t in range(NT):
                ins = SC.activation(zs[:, t], ys[:, t], ACT.Square, accum_out=rms[:, 0, t:t + 1])
            ins.then_inc(sem["rms_sq"], 1)
            act.wait_ge(sem["rms_sq"], upto("rms_sq", i, 2))
            SC.activation(rms[:, 1], rms[:, 0], ACT.Sqrt, scale=1.0 / INNER, bias=eps_ln[:, 0:1]).then_inc(sem["rms_std"], 1)
            for n in range(4):
                a, h = divmod(n, 2)
                act.wait_ge(sem["yt_ps"], upto("yt_ps", i, n + 1))
                SC.activation(y_t[:, a, h * HALF:(h + 1) * HALF], PB[n][:], ACT.Identity, scale=gnorm[:, a:a + 1]).then_inc(sem["yt_sb"], 1)
            yield
            yield

        def dve_ssm(dve, i, link):
            n64 = NT * HEADS
            dve.wait_ge(sem["t2"], upto("t2", i))
            yield from ln_stats(dve, i, 2, t0, link)
            yield PIECE
            dve.wait_ge(sem["rms_std"], upto("rms_std", i, 1))
            V.reciprocal(rms[:, 2], rms[:, 1]).then_inc(sem["rms_r"], 1)
            yield PIECE
            for _ in range(NT):
                yield PIECE
            link(V.tensor_tensor(t0[:], t0[:], u[:], ALU.add))
            dve.wait_ge(sem["z_sb"], upto("z_sb", i))
            dt3 = dtx[:, 0].rearrange("p (t h) -> p t h", h=HEADS)
            link(V.tensor_tensor(dt3, dtr[:], dt_bias[:].unsqueeze(1).to_broadcast([P, NT, HEADS]), ALU.add))
            V.scalar_tensor_tensor(dtx[:, 1], dtx[:, 0], -1.0, dtx[:, 0], ALU.mult, ALU.max).then_inc(sem["dt_abs"], 1)
            yield PIECE
            yield PIECE
            dve.wait_ge(sem["dt_exp"], upto("dt_exp", i))
            V.tensor_scalar(dtx[:, 3], dtx[:, 2], 1.0, None, ALU.add).then_inc(sem["dt_w"], 1)
            yield GAP["dt"]
            dve.wait_ge(sem["dt_ln"], upto("dt_ln", i))
            link(V.tensor_scalar(dtx[:, 3], dtx[:, 3], -1.0, None, ALU.add))
            link(V.tensor_scalar(dtx[:, 5], dtx[:, 3], 0.0, None, ALU.is_equal))
            link(V.tensor_tensor(dtx[:, 4], dtx[:, 4], dtx[:, 5], ALU.add))
            link(V.tensor_tensor(dtx[:, 3], dtx[:, 3], dtx[:, 5], ALU.add))
            link(V.reciprocal(dtx[:, 3], dtx[:, 3]))
            link(V.tensor_tensor(dtx[:, 4], dtx[:, 4], dtx[:, 3], ALU.mult))
            link(V.tensor_tensor(dtx[:, 4], dtx[:, 4], dtx[:, 2], ALU.mult))
            link(V.scalar_tensor_tensor(dtx[:, 0], dtx[:, 0], 0.0, dtx[:, 4], ALU.max, ALU.add))
            V.tensor_tensor(la[:], dt3, neg_a[:].unsqueeze(1).to_broadcast([P, NT, HEADS]), ALU.mult).then_inc(sem["la"], 1)
            dve.wait_ge(sem["xbc_sb"], upto("xbc_sb", i))
            for t in range(NT):
                ins = V.tensor_tensor(heads(ys[:, t]), heads(xbc[:, t, 0:INNER]), hb(dskip[:]), ALU.mult)
            link(ins)
            link(V.memset(state[:], 0.0))
            yield PIECE
            yield PIECE
            dve.wait_ge(sem["ecum"], upto("ecum", i))
            ec = ecum[:].rearrange("p a (t h) -> p a t h", h=HEADS)
            dte = dtx[:, 1].rearrange("p (t h) -> p t h", h=HEADS)
            link(V.tensor_tensor(dte, dt3, ec[:, 1], ALU.mult))
            for c in range(NT):
                if c:
                    dve.wait_ge(sem["ds_ps"], upto("ds_ps", i, c))
                    dve.wait_ge(sem["y_ps"], upto("y_ps", i, c))
                V.tensor_tensor(heads(xdt[:]), heads(xbc[:, c, 0:INNER]), hb(dt3[:, c]), ALU.mult)
                V.tensor_tensor(heads(xdr[:]), heads(xbc[:, c, 0:INNER]), hb(dte[:, c]), ALU.mult).then_inc(sem["xdr"], 1)
                dve.wait_ge(sem["decay"], upto("decay", i, c + 1))
                dve.wait_ge(sem["cbt"], upto("cbt", i, c + 1))
                V.tensor_tensor(mix[:], decay[:], PB[2][:, 0:P].unsqueeze(1).to_broadcast([P, HEADS, P]),
                                     ALU.mult).then_inc(sem["mix"], 1)
                yield PIECE
                dve.wait_ge(sem["y_ps"], upto("y_ps", i, c + 1))
                dve.wait_ge(sem["ds_ps"], upto("ds_ps", i, c + 1))
                V.tensor_tensor(ys[:, c], ys[:, c], PB[3][:, 0:INNER], ALU.add)
                V.tensor_tensor(heads(yoff[:]), heads(PB[3][:, INNER:2 * INNER]), hb(ec[:, 0, c]), ALU.mult)
                link(V.tensor_tensor(heads(state[:]), heads(state[:]), hb(ec[0:STATE, 2, c]), ALU.mult))
                V.tensor_tensor(ys[:, c], ys[:, c], yoff[:], ALU.add).then_inc(sem["y_sb"], 1)
                V.tensor_tensor(state[:], state[:], PB[2][0:STATE, 0:INNER], ALU.add).then_inc(sem["state"], 1)
                dve.wait_ge(sem["state"], upto("state", i, c + 1))
                yield PIECE
            dve.wait_ge(sem["y_sb"], upto("y_sb", i))
            link(V.tensor_tensor(ys[:], ys[:], zs[:], ALU.mult), "yn")
            yield PIECE
            yield GAP["rms"]
            dve.wait_ge(sem["rms_std"], upto("rms_std", i, 2))
            link(V.reciprocal(rms[:, 2], rms[:, 1]))
            for t in range(NT):
                dve.wait_ge(sem["o_ps"], upto("o_ps", i, t // 4 + 1))
                ins = V.scalar_tensor_tensor(t1[:, t], PB[t // 4][:, (t % 4) * P:(t % 4 + 1) * P], rms[:, 2, t:t + 1],
                                             t0[:, t], ALU.mult, ALU.add)
            ins.then_inc(sem["t3"], 1)
            dve.wait_ge(sem["t3"], upto("t3", i))
            yield PIECE

        W3, W2 = HID, 2 * HID

        def sp_e2(sp, i):
            for e in range(E8):
                if e >= 2:
                    sp.wait_ge(sem["y2_ps"], upto("y2_ps", i, 6 * (e - 1)))
                    settle(sp)
                s = "e2_in%d" % (e % 2)
                sp.dma_start(e2w[:, e % 2, 0:HID], A["moe2_w1_t"][e]).then_inc(sem[s], 16)
                sp.dma_start(e2w[:, e % 2, W3:W3 + HID], A["moe2_w3_t"][e]).then_inc(sem[s], 16)
                for k, m in enumerate(HTILES):
                    sp.dma_start(e2w[0:m, e % 2, W2 + k * C:W2 + (k + 1) * C],
                                      A["moe2_w2_t"][e, k * P:k * P + m]).then_inc(sem[s], 16)

        def pe_moe2(pe, i):
            yield
            pe_ln(pe, i, 3)
            yield
            pe_logits(pe, i, 1, router2)
            yield
            pe.wait_ge(sem["gated"], upto("gated", i, 2))
            for h in range(2):
                T.matmul(PB[2 + h][:], ident[:], flat4(t1, h), start=True, stop=False)

            def y_part(n):
                eh, k = divmod(n, 3)
                e, h = divmod(eh, 2)
                m = HTILES[k]
                pe.wait_ge(sem["hh"], upto("hh", i, n + 1))
                for t in range(4):
                    ins = T.matmul(PB[2 + h][:, t * P:(t + 1) * P], gated_h[0:m, n % SLOTS, t * P:(t + 1) * P],
                                   e2w[0:m, e % 2, W2 + k * C:W2 + (k + 1) * C], start=False,
                                   stop=(e == E8 - 1 and k == 2 and t == 3))
                ins.then_inc(sem["y2_ps"], 1)

            def gate_u(eh):
                pe.wait_ge(sem["gate_diag"], upto("gate_diag", i, eh + 1))
                if eh:
                    pe.wait_ge(sem["h3_sb"], upto("h3_sb", i, 3 * eh - 1))
                for t in range(4):
                    ins = T.matmul(GB[3 * eh % 2][:, t * P:(t + 1) * P], u[:, 4 * (eh % 2) + t],
                                   gate_diag[:, eh % 2, t * P:(t + 1) * P], start=True, stop=True)
                ins.then_inc(sem["gb2"], 1)

            gate_u(0)
            for n in range(48 + LAG2):
                if n < 48:
                    eh, k = divmod(n, 3)
                    e, h = divmod(eh, 2)
                    m = HTILES[k]
                    if k == 0:
                        pe.wait_ge(sem["e2_in%d" % (e % 2)], upto("e2_in%d" % (e % 2), i, 80 * (e // 2 + 1)))
                    if n:
                        pe.wait_ge(sem["silu"], upto("silu", i, n))
                    T.matmul(PB[0][0:m, :], e2w[:, e % 2, k * P:k * P + m], uhalf(h), start=True, stop=True).then_inc(sem["h1_ps"], 1)
                    if n >= 2:
                        pe.wait_ge(sem["h3_sb"], upto("h3_sb", i, n - 1))
                    if k == 0:
                        pe.wait_ge(sem["gu"], upto("gu", i, eh + 1))
                    T.matmul(GB[n % 2][0:m, :], e2w[:, e % 2, W3 + k * P:W3 + k * P + m], gated_u[:, eh % 2],
                                  start=True, stop=True).then_inc(sem["h3_ps"], 1)
                if n >= LAG2:
                    y_part(n - LAG2)
                if n < 48 and k == 2 and eh + 1 < 16:
                    gate_u(eh + 1)
                yield

        def act_moe2(act, i):
            yield from act_ln(act, i, 3)
            yield
            act_route(act, i, 1)
            yield

            def gate_diag_of(eh):
                e, h = divmod(eh, 2)
                if eh >= 2:
                    act.wait_ge(sem["gb2"], upto("gb2", i, eh - 1))
                for t in range(4):
                    ins = SC.activation(gate_diag[:, eh % 2, t * P:(t + 1) * P], ident[:], ACT.Copy,
                                        scale=gates[:, 4 * h + t, e:e + 1])
                ins.then_inc(sem["gate_diag"], 1)

            def gate_u(eh):
                act.wait_ge(sem["gb2"], upto("gb2", i, eh + 1))
                if eh >= 2:
                    act.wait_ge(sem["h3_ps"], upto("h3_ps", i, 3 * (eh - 1)))
                SC.activation(gated_u[:, eh % 2], GB[3 * eh % 2][:], ACT.Identity).then_inc(sem["gu"], 1)

            act.wait_ge(sem["gated"], upto("gated", i, 2))
            gate_diag_of(0)
            gate_diag_of(1)
            gate_u(0)
            for n in range(48 + LAG2):
                if n < 48:
                    m = HTILES[n % 3]
                    act.wait_ge(sem["h1_ps"], upto("h1_ps", i, n + 1))
                    if n >= SLOTS:
                        act.wait_ge(sem["y2_ps"], upto("y2_ps", i, n - SLOTS + 1))
                    SC.activation(act_h[0:m, n % SLOTS], PB[0][0:m, :], ACT.Silu).then_inc(sem["silu"], 1)
                    eh, k = divmod(n, 3)
                    if k == 1 and 1 <= eh < 15:
                        gate_diag_of(eh + 1)
                    act.wait_ge(sem["h3_ps"], upto("h3_ps", i, n + 1))
                    if n >= H3_SLOTS:
                        act.wait_ge(sem["hh"], upto("hh", i, n - H3_SLOTS + 1))
                    SC.activation(h3_s[0:m, n % H3_SLOTS], GB[n % 2][0:m, :], ACT.Identity).then_inc(sem["h3_sb"], 1)
                    if k == 2 and eh < 15:
                        gate_u(eh + 1)
                yield
            for h in range(2):
                act.wait_ge(sem["y2_ps"], upto("y2_ps", i, 45 + 3 * h))
                SC.activation(flat4(t0, h), PB[2 + h][:], ACT.Identity).then_inc(sem["out_sb"], 1)

        def dve_moe2(dve, i, link):
            yield from ln_stats(dve, i, 3, t1, link)
            yield PIECE
            yield from dve_route(dve, i, 1, link)
            yield PIECE
            for n in range(48 + LAG2):
                if n >= 2 and n - 2 < 48:
                    n -= 2
                    m, slot = HTILES[n % 3], n % SLOTS
                    dve.wait_ge(sem["silu"], upto("silu", i, n + 1))
                    dve.wait_ge(sem["h3_sb"], upto("h3_sb", i, n + 1))
                    V.tensor_tensor(gated_h[0:m, slot], act_h[0:m, slot], h3_s[0:m, n % H3_SLOTS], ALU.mult).then_inc(sem["hh"], 1)
                yield PIECE

        def sp_out(sp, i):
            sp.wait_ge(sem["out_sb"], upto("out_sb", i))
            settle(sp)
            sp.dma_start(A["out"][bass.ds(i, 1)].rearrange("a (t r) w c -> (a r w) t c", t=NT), t0[:]).then_inc(sem["out"], 16)

        SECOND = [
            7.2, 6.4, 4, 6, 5.4, 6.3, 5.9, 6.1, 5.9, 5.9, 18.9, 7.9, 5.6, 5, 5, 2.9, 6.5, 6.7, 13.7, 6, 3, 7.3,
            9.2, 3.7, 3, 3.5, 3.1, 4.3, 3.8, 3.7, 3.6, 3.1, 3.4, 3.9, 3.4, 3.2, 3.2, 3, 3, 7.5, 6.3, 8.3, 5, 5,
            5, 5, 5, 5, 5, 5, 15.1, 3, 8.4, 3, 10.9, 9.3, 4.4, 7.6, 4.3, 6.3, 4.3, 5.8, 4.3, 6.4, 4.4, 7.2, 4.4,
            6.9, 5.1, 6.6, 10.1, 11.2, 6.5, 6.5, 13.6, 4.9, 15.1, 5.5, 6.2, 5.6, 4.1, 3, 3.4, 3.8, 3.3, 4.4,
            3.3, 3.2, 7.8, 4.8, 3.1, 3.4, 3.2, 4.2, 3.2, 3.3, 3, 3.2, 3.3, 3.4, 3.4, 3.7, 3.4, 3.1, 3.4, 4.1,
            3.3, 3.3, 3.2, 3.1, 3.4, 3.1, 3.3, 3.5, 3, 3.3, 3.3, 3.1, 3.3, 3.3, 3.1, 3.3, 3.4, 3.4, 3.1, 3.1, 3,
            3.1
        ]
        FILL_SECOND = [
            3.4, 1.8, 0.6, 0.9, 1.5, 3.3, 4.6, 2.6, 2.6, 2.7, 10.9, 13.4, 2, 0.8, 0.8, 0.7, 2.8, 3.1, 9.6, 0.9,
            0.5, 9, 4.3, 3.5, 1.8, 2.6, 1.8, 1.3, 4.6, 2.1, 1.6, 1.6, 1.4, 3.1, 2.2, 3.6, 0.9, 0.5, 0.5, 7.5,
            1.8, 2.2, 0.7, 0.7, 0.7, 0.7, 0.7, 0.7, 0.7, 0.7, 21.7, 0.5, 7.1, 0.5, 6.2, 4.2, 2.7, 5.4, 3.3, 3.9,
            1.7, 3.2, 1.9, 4.2, 1.3, 5.2, 3.1, 3.3, 3.9, 4.9, 1.8, 3.1, 2.1, 1.8, 9.5, 0.5, 4.1, 3.1, 2, 4, 2.3,
            1, 1.1, 2.9, 1.4, 3.7, 1.3, 1, 2.3, 6.4, 1.5, 1.8, 0.7, 5.9, 2, 1.5, 1, 1.8, 1.1, 3.3, 2, 2.9, 2, 1,
            1.5, 5.6, 2.1, 1.7, 1.3, 1, 1.2, 0.7, 0.5, 1, 0.9, 0.8, 0.9, 1.4, 0.8, 1, 1.5, 1.2, 1.6, 2.2, 1.3,
            0.6, 0.5, 0.8
        ]
        FIRST = [
            5.8, 3.9, 5.8, 18, 1.7, 7, 7, 7, 7, 7, 7, 7, 7, 7, 7, 7, 7, 7, 7, 7, 7, 7, 7, 7, 7, 7, 7, 7, 7, 6,
            4, 6, 2.3, 2.3, 2.3, 2.3
        ]
        FILL_FIRST = [
            6.9, 8.7, 1.2, 2.7, 4.5, 1.1, 1.1, 1.1, 1.1, 1.1, 1.1, 1.1, 1.1, 1.1, 1.1, 1.1, 1.1, 1.1, 1.1, 1.1,
            1.1, 1.1, 1.1, 1.1, 1.1, 1.1, 1.1, 1.1, 1.1, 4.3, 2.4, 5.1, 0.3, 0.3, 0.3, 0.3
        ]
        assert len(SECOND) == (8 + NT) + (4 + 2 * E8 + LAG1) + (9 + 3 * NT) + (3 + 6 * E8 + LAG2)
        assert len(FIRST) == 5 + NG + 3 + SORT_T

        def order():
            out, a, b, ta, tb = [], 0, 0, 0.0, 0.0
            while a < len(FIRST) or b < len(SECOND):
                fa = (ta + FIRST[a] / 2) / sum(FIRST) if a < len(FIRST) else 9
                fb = (tb + SECOND[b] / 2) / sum(SECOND) if b < len(SECOND) else 9
                if fa < fb:
                    out.append(("first", a))
                    ta, a = ta + FIRST[a], a + 1
                else:
                    out.append(("second", b))
                    tb, b = tb + SECOND[b], b + 1
            return out

        def fills():
            fill = [(FILL_FIRST if p == "first" else FILL_SECOND)[n] for p, n in order()]
            return np.cumsum(fill) / sum(fill)

        def interleave(first, second):
            for part, _ in order():
                gen = first if part == "first" else second
                if gen is not None:
                    next(gen)
            for gen in (first, second):
                assert gen is None or next(gen, None) is None and next(gen, "end") == "end"

        def pe_second(pe, i):
            yield from pe_att(pe, i)
            yield from pe_moe1(pe, i)
            yield from pe_ssm(pe, i)
            yield from pe_moe2(pe, i)

        def pe_first(pe, i):
            yield from pe_pre(pe, i)
            yield from pe_corr(pe, i, 0)

        def act_second(act, i):
            yield from act_att(act, i)
            yield from act_moe1(act, i)
            yield from act_ssm(act, i)
            yield from act_moe2(act, i)

        def act_first(act, i):
            yield from act_pre(act, i)
            yield from act_corr(act, i, 0)

        def dve_second(dve, i):
            dve.wait_ge(sem["out"], upto("out", i, 16))
            link = Chain(dve, "dve_post", i)
            dve.wait_ge(sem["ranked"], upto("ranked", i))
            link(V.tensor_copy(t0[:], x2_tok[:]), "t_in")
            yield from dve_att(dve, i, link)
            yield from dve_moe1(dve, i, link)
            yield from dve_ssm(dve, i, link)
            yield from dve_moe2(dve, i, link)
            link.end()

        def dve_sorts(dve, i):
            link = Chain(dve, "dve_sort", i)
            for h in range(2):
                yield from dve_sort(dve, i, h, link)
            link.end()

        SORT_STEPS = 2 * 100

        def dve_body(dve, i, first, sort, second):
            gens = dict(first=dve_pre(dve, i + 1) if first else None, second=dve_second(dve, i - 1) if second else None)
            sorts, steps = (dve_sorts(dve, i), 0) if sort else (None, 0)

            def step():
                nonlocal steps
                if sorts is not None and steps < SORT_STEPS:
                    next(sorts)
                    steps += 1

            if sort:
                step()
            for (part, n), share in zip(order(), fills()):
                while sort and steps < min(share, 1) * SORT_STEPS:
                    step()
                gen = gens[part]
                while gen is not None and (gap := next(gen)) is not PIECE:
                    for _ in range(gap):
                        step()
            if sort:
                assert next(sorts, "end") == "end" and steps == SORT_STEPS
            for gen in gens.values():
                assert gen is None or next(gen, "end") == "end"

        def whole(gen):
            for _ in gen:
                pass

        def run(eng, body):
            body(-1, True, False, False)
            body(0, True, True, False)
            if IMGS > 2:
                with eng.Fori(1, IMGS - 1) as i:
                    body(i, True, True, True)
            body(IMGS - 1, False, True, True)
            body(IMGS, False, False, True)

        block = ctx.enter_context(nc.Block())

        @block.sync
        def _(sp):
            sp_x(sp, 0)
            sp_load(sp)
            sp_zero_quads(sp)
            others_prep(sp)
            sp.sem_inc(sem["out"], 16)

            def body(i, first, sort, second, more):
                if first:
                    sp_pre(sp, i + 1)
                if second:
                    sp_e1(sp, i - 1)
                    sp_e2(sp, i - 1)
                if more:
                    sp_x(sp, i + 2)
                if second:
                    sp_out(sp, i - 1)

            body(-1, True, False, False, True)
            body(0, True, True, False, True)
            if IMGS > 3:
                with sp.Fori(1, IMGS - 2) as i:
                    body(i, True, True, True, True)
            if IMGS > 2:
                body(IMGS - 2, True, True, True, False)
            body(IMGS - 1, False, True, True, False)
            body(IMGS, False, False, True, False)
            sp.wait_ge(sem["out"], 16 * (IMGS + 1))

        @block.scalar
        def _(act):
            act.wait_ge(prep, 1)

            def body(i, first, sort, second):
                if sort:
                    act.wait_ge(sem["t_in"], upto("t_in", i, 0))
                    SC.activation(x2_tok[:], x1_tok[:], ACT.Identity).then_inc(sem["x2_copy"], 1)
                    whole(act_corr(act, i, 1))
                interleave(act_first(act, i + 1) if first else None, act_second(act, i - 1) if second else None)

            run(act, body)

        @block.vector
        def _(dve):
            dve_prep(dve)
            run(dve, lambda i, first, sort, second: dve_body(dve, i, first, sort, second))

        @block.gpsimd
        def _(pool):
            others_prep(pool)

            def body(i, first, sort, second):
                if first:
                    whole(pool_pre(pool, i + 1))

            run(pool, body)

        @block.tensor
        def _(pe):
            pe.wait_ge(early, 16 * 2)

            def body(i, first, sort, second):
                if sort:
                    whole(pe_corr(pe, i, 1))
                interleave(pe_first(pe, i + 1) if first else None, pe_second(pe, i - 1) if second else None)

            run(pe, body)



CHAIN_N = dict(dve_pre=19, dve_post=116, dve_sort=112)


def constants():
    k, j = np.arange(P)[:, None], np.arange(P)[None, :]
    f = np.float32
    key, q = np.arange(KEYS)[None, :], np.arange(P)[:, None] + BACK
    band = np.stack([np.where((key <= q) & (key > q - w), 0.0, -NEG) for w in WINDOWS], 1)
    tok = np.arange(TOK).reshape(NT, P).T[:, :, None]
    tap = np.arange(TAPS)[None, None, :]
    ys, xs = tok // WIDTH + tap // 3, tok % WIDTH + tap % 3
    return dict(
        c_ident=np.eye(P, dtype=f), c_gavg=((k // GROUP == j // GROUP) / GROUP).astype(f),
        c_tri=(k <= j).astype(f), c_later=(k > j).astype(f),
        c_future=np.where(j < k, NEG, 0.0).astype(f), c_band=band.astype(f),
        c_base=np.stack([ys.reshape(P, -1), xs.reshape(P, -1)], 1).astype(f),
        c_rev=np.broadcast_to(E8 - np.arange(E8), (P, E8)).astype(f),
  )


def layouts(a):
    t = np.ascontiguousarray
    w_in = a["L3_attn_W_in"]
    conv_b = a["L3_attn_conv_b"]
    out = {n: t(a[n]) for n in (
        "x", "L0_conv_om_kernel", "L0_conv_om_bias", "L0_conv_kernel", "L0_conv_bias", "L2_attn_Wq", "L2_attn_bq",
        "L2_attn_Wk", "L2_attn_bk", "L2_attn_Wv", "L2_attn_bv", "L2_attn_Wo", "L2_attn_bo", "L2_ffn_w1", "L2_ffn_w2",
        "L2_ffn_b2", "L3_attn_conv_b", "L3_attn_dt_bias", "L3_attn_A_log", "L3_attn_Dp", "L3_attn_norm_w")}
    out.update(
        router1_t=t(a["L2_ffn_router_w"].T), router2_t=t(a["L3_ffn_router_w"].T), b1_t=t(a["L2_ffn_b1"].T),
        w_zdt_t=t(np.concatenate([w_in[:INNER], w_in[INNER + XBC:]]).T), w_xbc_t=t(w_in[INNER:INNER + XBC].T),
        conv_w_t=t(a["L3_attn_conv_w"].T),
        gnorm_t=t(a["L3_attn_gnorm_w"].reshape(2, P).T),
        w_out_t=t(a["L3_attn_W_out"].T.reshape(2, P, C).transpose(1, 0, 2)),
        moe2_w1_t=t(a["L3_ffn_w1"].transpose(0, 2, 1)), moe2_w3_t=t(a["L3_ffn_w3"].transpose(0, 2, 1)),
        moe2_w2_t=t(a["L3_ffn_w2"].transpose(0, 2, 1)),
  )
    return out


def kernel(**inputs):
    import concourse.bacc as _bacc
    from concourse.bass_utils import run_bass_kernel_spmd as _run

    arrays = {**constants(), **layouts({n: np.asarray(v) for n, v in inputs.items()})}
    nc = _bacc.Bacc("TRN2", target_bir_lowering=False, num_devices=1)
    A = {n: nc.dram_tensor(n, a.shape, mybir.dt.from_np(a.dtype), kind="ExternalInput").ap()
         for n, a in arrays.items()}
    A["out"] = nc.dram_tensor("out", (IMAGES, HEIGHT, WIDTH, C), mybir.dt.float32, kind="ExternalOutput").ap()
    build(nc, A)
    r = _run(nc, [arrays], core_ids=[0])
    return r.results[0]["out"]
```
